# Optimizing a Trainium2 kernel written in Bass

```python
import numpy as np
import jax
import jax.numpy as jnp

def _softmax(x, axis=-1):
    return jax.nn.softmax(x, axis=axis)

def _gelu(x):
    return jax.nn.gelu(x, approximate=True)

def _silu(x):
    return jax.nn.silu(x)

def _sigmoid(x):
    return jax.nn.sigmoid(x)

def _layernorm(x, axis=-1, eps=1e-05):
    m = jnp.mean(x, axis=axis, keepdims=True)
    v = jnp.var(x, axis=axis, keepdims=True)
    return (x - m) / jnp.sqrt(v + eps)

def _scatter_add(tgt, idx, src, axis=0):
    return tgt.at[idx].add(src)

def _segment_sum(src, seg, n):
    return jax.ops.segment_sum(src, seg, n)
kernel_name = 'mk_xattn_ffn_d1_seqx_r8_2c07eb'

def setup_inputs(seed: int=0):
    np.random.seed(seed)
    _w = jnp.asarray

    def _rec_inputs():
        import jax
        import jax.numpy as jnp
        _rk = jax.random.key(seed)
        x = 7.22e-05 + 1 * jax.random.normal(jax.random.fold_in(_rk, 1), (16, 56, 256), jnp.float32)
        _lenS = 56 - jax.random.randint(jax.random.fold_in(_rk, 7), (16,), 0, max(1, 56 // 4) + 1, jnp.int32)
        _lenS2 = 1500 - jax.random.randint(jax.random.fold_in(_rk, 8), (16,), 0, max(1, 1500 // 4) + 1, jnp.int32)
        _ctx_512P = jax.random.normal(jax.random.fold_in(_rk, 11), (16, 16, 64), jnp.float32)
        _ctx_512c = jax.random.dirichlet(jax.random.fold_in(_rk, 511), 0.3 * jnp.ones((16,), jnp.float32), (16, 1500))
        _ctx_512t = jnp.einsum('bsk,bkd->bsd', _ctx_512c, _ctx_512P)
        _ctx_512t = _ctx_512t * jax.lax.rsqrt(jnp.mean(jnp.square(_ctx_512t)) + 1e-12) * 0.953939
        ctx_512 = -0.000514642 + 1.00011 * (_ctx_512t + 0.3 * jax.random.normal(jax.random.fold_in(_rk, 611), (16, 1500, 64), jnp.float32))
        return (x, ctx_512)
    x, ctx_512 = _rec_inputs()

    def _L0_xattn_setup():
        import jax, jax.numpy as jnp
        import numpy as np
        B, S, H, NH, L = (2, 256, 256, 16, 64)
        HD = H // NH
        key = jax.random.key(seed)
        k1, k2, k3, k4, k5 = jax.random.split(key, 5)
        scale = 0.02
        return {'q': jax.random.normal(k1, (B, S, H), dtype=jnp.float32), 'latent_kv': jax.random.normal(k2, (B, S, L), dtype=jnp.float32), 'Wq': jax.random.normal(k3, (H, H), dtype=jnp.float32) * scale, 'Wkv_expand': jax.random.normal(k4, (2 * H, L), dtype=jnp.float32) * scale, 'Wout': jax.random.normal(k5, (H, H), dtype=jnp.float32) * scale}
    _L0_xattn_all = _L0_xattn_setup()
    _L0_xattn_in = {k: v for k, v in _L0_xattn_all.items() if k in ('Wq', 'Wkv_expand', 'Wout')}
    del _L0_xattn_all

    def _L0_ffn_setup():
        import jax, jax.numpy as jnp
        import numpy as np
        EPS = 1e-05

        def _quant_weight(w):
            scale = jnp.mean(jnp.abs(w)) + EPS
            wq = jnp.clip(jnp.round(w / scale), -1.0, 1.0)
            return (wq, scale)

        def _quant_act(x):
            s = jnp.max(jnp.abs(x), axis=-1, keepdims=True) / 127.0 + EPS
            xq = jnp.clip(jnp.round(x / s), -128.0, 127.0)
            return (xq, s)

        def _qlinear(x, w):
            wq, ws = _quant_weight(w)
            xq, xs = _quant_act(x)
            y = jnp.einsum('bsi,oi->bso', xq, wq)
            return y * xs * ws
        key = jax.random.key(seed)
        k1, k2, k3, k4 = jax.random.split(key, 4)
        H, I = (256, 1024)
        x = jax.random.normal(k1, (4, 512, H), dtype=jnp.float32)
        w_gate = jax.random.normal(k2, (I, H), dtype=jnp.float32) * (1.0 / np.sqrt(H))
        w_up = jax.random.normal(k3, (I, H), dtype=jnp.float32) * (1.0 / np.sqrt(H))
        w_down = jax.random.normal(k4, (H, I), dtype=jnp.float32) * (1.0 / np.sqrt(I))
        return {'x': x, 'w_gate': w_gate, 'w_up': w_up, 'w_down': w_down}
    _L0_ffn_all = _L0_ffn_setup()
    _L0_ffn_in = {k: v for k, v in _L0_ffn_all.items() if k in ('w_gate', 'w_up', 'w_down')}
    del _L0_ffn_all
    return {'x': x, 'ctx_512': ctx_512, 'L0_xattn_Wq': _L0_xattn_in['Wq'], 'L0_xattn_Wkv_expand': _L0_xattn_in['Wkv_expand'], 'L0_xattn_Wout': _L0_xattn_in['Wout'], 'L0_ffn_w_gate': _L0_ffn_in['w_gate'], 'L0_ffn_w_up': _L0_ffn_in['w_up'], 'L0_ffn_w_down': _L0_ffn_in['w_down']}

def reference(x, ctx_512, L0_xattn_Wq, L0_xattn_Wkv_expand, L0_xattn_Wout, L0_ffn_w_gate, L0_ffn_w_up, L0_ffn_w_down):
    import jax
    import jax.numpy as jnp

    def _L0_xattn_ref(q, latent_kv, Wq, Wkv_expand, Wout):
        import jax, jax.numpy as jnp
        import numpy as np
        B, S, H, NH, L = (2, 256, 256, 16, 64)
        HD = H // NH
        b, sq, _ = q.shape
        sk = latent_kv.shape[1]
        qp = q @ Wq.T
        kv = latent_kv @ Wkv_expand.T
        k, v = jnp.split(kv, 2, axis=-1)
        qh = qp.reshape(b, sq, NH, HD).transpose(0, 2, 1, 3)
        kh = k.reshape(b, sk, NH, HD).transpose(0, 2, 1, 3)
        vh = v.reshape(b, sk, NH, HD).transpose(0, 2, 1, 3)
        inv_sqrt_d = 1.0 / jnp.sqrt(jnp.float32(HD))
        scores = jnp.einsum('bhqd,bhkd->bhqk', qh, kh) * inv_sqrt_d
        causal = jnp.tril(jnp.ones((sq, sk), dtype=bool))
        scores = jnp.where(causal, scores, jnp.finfo(scores.dtype).min)
        attn = jax.nn.softmax(scores, axis=-1)
        out = jnp.einsum('bhqk,bhkd->bhqd', attn, vh)
        out = out.transpose(0, 2, 1, 3).reshape(b, sq, H)
        return out @ Wout.T

    def _L0_ffn_ref(x, w_gate, w_up, w_down):
        import jax, jax.numpy as jnp
        import numpy as np
        EPS = 1e-05

        def _quant_weight(w):
            scale = jnp.mean(jnp.abs(w)) + EPS
            wq = jnp.clip(jnp.round(w / scale), -1.0, 1.0)
            return (wq, scale)

        def _quant_act(x):
            s = jnp.max(jnp.abs(x), axis=-1, keepdims=True) / 127.0 + EPS
            xq = jnp.clip(jnp.round(x / s), -128.0, 127.0)
            return (xq, s)

        def _qlinear(x, w):
            wq, ws = _quant_weight(w)
            xq, xs = _quant_act(x)
            y = jnp.einsum('bsi,oi->bso', xq, wq)
            return y * xs * ws
        gate = jax.nn.silu(_qlinear(x, w_gate))
        up = _qlinear(x, w_up)
        return _qlinear(gate * up, w_down)
    x = x + _L0_xattn_ref(_layernorm(x, axis=-1), ctx_512, L0_xattn_Wq, L0_xattn_Wkv_expand, L0_xattn_Wout)
    x = x + _L0_ffn_ref(_layernorm(x, axis=-1), L0_ffn_w_gate, L0_ffn_w_up, L0_ffn_w_down)
    return x

_drawn_inputs = setup_inputs


def setup_inputs(seed=0):
    import zlib

    import numpy as np

    out = dict(_drawn_inputs(seed))
    spreads = {}
    factors = {'L0_xattn_Wq': 62.609}
    for name, (base, spread) in spreads.items():
        noise = np.random.default_rng([zlib.crc32(name.encode()), seed]).standard_normal(out[name].shape)
        drawn = base * np.exp(spread * noise) if base else spread * noise
        out[name] = jnp.asarray(drawn.astype(out[name].dtype))
    for name, factor in factors.items():
        out[name] = (out[name] * factor).astype(out[name].dtype)
    return out
```

```python
from contextlib import ExitStack

import concourse.bass as bass
from concourse import mybir

F32, BF16 = mybir.dt.float32, mybir.dt.bfloat16
ALU = mybir.AluOpType
ACT = mybir.ActivationFunctionType
AX_X = mybir.AxisListType.X

P = 128
EPS = 1e-5
NEG = -3.0e38
MAGIC = 1.5 * 2.0 ** 23


def xattn_ffn(nc, x, ctx_512, wq, wkv, wout, w_gate, w_up, w_down, out):
    B, S, C = x.shape
    L = ctx_512.shape[2]
    I = w_gate.shape[0]
    HD = 16
    NH = C // HD
    T = B * S
    NT = T // P
    HALVES = C // P
    HH = NH // HALVES
    NP = B // 2
    NU = NP * HALVES
    Q = 64
    HP = HH // 2
    CT = 2 * 2 * S
    KT = 4 * 2 * S
    NQC, NKC = T // CT, T // KT
    VB = 4
    NV = B // VB
    NC8 = I // P
    GC = 512
    NG = I // GC
    WN = I * C
    WF = WN // P
    PIECE = 512
    NPIECE = WF // PIECE
    SCALE = float(HD) ** -0.5
    assert T % P == 0 and S <= Q and HALVES == 2 and NG == 2 and KT <= 512 and NT == 7

    LAG_T, LAG_V = 3, 4
    OP0 = 8
    XT0 = OP0 + 2
    GU0 = 18
    HT0 = GU0 + 2
    SLOTS = HT0 + NT
    ABS0 = 3
    TERN0 = ABS0 + 3

    misc = {s: [] for s in range(-1, SLOTS)}
    misc[-1] = [("wkvT", 0), ("ctxT", 0), ("ctxT", 1), ("k", 0, 0), ("k", 0, 1), ("wqT", 0),
                ("xT", 0), ("xT", 1), ("q", 0)]
    misc[0] += [("k", 1, 0), ("k", 1, 1)]
    misc[1] += [("xT", 2), ("xT", 3)]
    misc[2] += [("q", 1)]
    misc[3] += [("v", 0), ("xT", 4), ("xT", 5)]
    misc[4] += [("woT", 0)]
    misc[5] += [("q", 2), ("xT", 6)]
    misc[6] += [("v", 1)]
    misc[7] += [("q", 3)]
    misc[9] += [("v", 2)]
    misc[13] += [("v", 3)]
    for w in range(3):
        misc[ABS0 + w + 1] += [("mean", w)]
        for k in range(2):
            misc[TERN0 + 4 + 2 * w + k] += [("wT", w, k)]
    for u in range(NU):
        misc[u + LAG_V] += [("pv", u)]
    for t in range(NT):
        misc[XT0 + 2 * t] += [("xqT", t)]
    misc_no = {}
    for s in range(-1, SLOTS):
        for job in misc[s]:
            misc_no[job] = len(misc_no)

    with ExitStack() as ctx:
        def sb(name, shape, dt=F32):
            return ctx.enter_context(nc.sbuf_tensor(name, shape, dt))

        def sem(name):
            return ctx.enter_context(nc.semaphore(name))

        x_sb = sb("x_sb", [P, NT, C])
        ctx_sb = sb("ctx_sb", [2 * S, NP, L])
        wq_sb = sb("wq_sb", [P, HALVES, C])
        wkv_sb = sb("wkv_sb", [P, 4, L])
        wo_sb = sb("wo_sb", [P, HALVES, C])
        wf_sb = sb("wf_sb", [P, 3, WF])
        xn_sb = sb("xn_sb", [P, 4, C])
        xnT = sb("xnT", [P, HALVES, T])
        wqT = sb("wqT", [P, HALVES, C])
        woT = sb("woT", [P, HALVES, C])
        wkvT = sb("wkvT", [L, 2 * C])
        ctxT = sb("ctxT", [L, T + Q - S])
        kT = sb("kT", [P, NKC, HALVES, KT])
        k_wide = sb("k_wide", [P, HALVES, HH, T])
        qT = sb("qT", [P, HALVES, B, Q])
        v_wide = sb("v_wide", [P, B, NH // 2, 2 * HD])
        soft = sb("soft", [P, 3, HH, S])
        p_norm = sb("p_norm", [P, 3, HH, Q])
        pT = sb("pT", [P, 2, HP, P])
        attnT = sb("attnT", [P, HALVES, T])
        mx = sb("mx", [P, 3, HH])
        den = sb("den", [P, 3, HH])
        rden = sb("rden", [P, 3, HH])
        ident = sb("ident", [P, P])
        ident_b = sb("ident_b", [P, P], BF16)
        sel2 = sb("sel2", [P, P], BF16)
        causal = sb("causal", [P, S], BF16)
        head_mask = sb("head_mask", [P, HH])
        minus_half = sb("minus_half", [P, 1])
        mean_w = sb("mean_w", [P, P])
        stats = sb("stats", [P, 2 * NT, 6])
        mv = sb("mv", [P, 2 * NT, 2])
        veps = sb("veps", [P, 2 * NT])
        rstd = sb("rstd", [P, 2 * NT])
        y_sb = sb("y_sb", [P, 2, C])
        y_int = sb("y_int", [P, 2, C])
        xq_b = sb("xq_b", [P, 2, C], BF16)
        xqT = sb("xqT", [P, NT, HALVES, P], BF16)
        amax = sb("amax", [P, 2, NT])
        s_tok = sb("s_tok", [P, 2, NT])
        r_tok = sb("r_tok", [P, 2, NT])
        s_out = sb("s_out", [P, 3, NT])
        asum = sb("asum", [P, 3])
        w_scale = sb("w_scale", [P, 3])
        w_thr = sb("w_thr", [P, 2, 3])
        pos = sb("pos", [P, 2, PIECE], BF16)
        neg = sb("neg", [P, 2, PIECE], BF16)
        tern = sb("tern", [P, 3, WF], BF16)
        wT = sb("wT", [P, 2, HALVES, I], BF16)
        wdT = sb("wdT", [P, NC8, C], BF16)
        kw = k_wide[:, :, :, :].rearrange("p a b c -> p (a b c)")
        g_sb = kw[:, 0:2 * I].rearrange("p (n i) -> p n i", n=2)
        h_sb = kw[:, 2 * I:5 * I].rearrange("p (n i) -> p n i", n=3)
        h_int = kw[:, 5 * I:7 * I].rearrange("p (n i) -> p n i", n=2)
        hq_b = kw[:, 7 * I:8 * I].bitcast(BF16).rearrange("p (n i) -> p n i", n=2)
        hT = kw[:, 8 * I:9 * I].bitcast(BF16).rearrange("p (n c t) -> p n c t", n=2, c=NC8)
        o_sb = kw[:, 9 * I:9 * I + NT * C].rearrange("p (t c) -> p t c", t=NT)

        banks = [ctx.enter_context(nc.psum_tensor(f"bank{i}", [P, 512], F32)) for i in range(8)]
        SC, TR, MI, OPB = banks[0:3], banks[3:5], banks[5:7], banks[7]

        x_parts = [(0, 2), (2, 4), (4, NT)]
        x_in = [sem(f"x_in{i}") for i in range(len(x_parts))]
        ctx_in, wkv_in, wq_in, wo_in = sem("ctx_in"), sem("wkv_in"), sem("wq_in"), sem("wo_in")
        wf_in = [sem(f"wf_in{i}") for i in range(3)]
        out_done = sem("out_done")
        const_ready = sem("const_ready")
        pads_ready = sem("pads_ready")
        dve_chain = sem("dve_chain")
        var_ready = sem("var_ready")
        rstd_ready = sem("rstd_ready")
        xn_ready = sem("xn_ready")
        kw_dve, kw_pool = sem("kw_dve"), sem("kw_pool")
        misc_written, misc_read = sem("misc_written"), sem("misc_read")
        scores_written, sub_ready = sem("scores_written"), sem("sub_ready")
        exp_ready, rden_ready, pn_ready = sem("exp_ready"), sem("rden_ready"), sem("pn_ready")
        tr_written, tr_read = sem("tr_written"), sem("tr_read")
        op_written, op_read = sem("op_written"), sem("op_read")
        y_ready = sem("y_ready")
        yint_ready = sem("yint_ready")
        xq_ready = sem("xq_ready")
        asum_ready = sem("asum_ready")
        posneg_ready, tern_ready = sem("posneg_ready"), sem("tern_ready")
        gu_written, silu_ready, h_ready = sem("gu_written"), sem("silu_ready"), sem("h_ready")
        gu_scale_ready = sem("gu_scale_ready")
        r_ready = sem("r_ready")
        hint_ready, hq_ready = sem("hint_ready"), sem("hq_ready")
        o_ready = sem("o_ready")

        CONSTS = ["ident", "minus_half", "head_mask", "sel2", "causal", "ident_b", "v_zero", "mean_w"]

        def const(eng, name):
            eng.wait_ge(const_ready, CONSTS.index(name) + 1)

        def x_part(t):
            return next(i for i, (a, b) in enumerate(x_parts) if a <= t < b)

        KW_DVE = [(hf, h) for hf in range(HALVES) for h in range(5)]
        KW_POOL = [(hf, h) for hf in range(HALVES) for h in range(5, HH)]

        x_v = x.rearrange("b s c -> (b s) c").rearrange("(t p) c -> p t c", p=P)
        out_v = out.rearrange("b s c -> (b s) c").rearrange("(t p) c -> p t c", p=P)

        block = ctx.enter_context(nc.Block())

        @block.sync
        def _(sp):
            for i, (a, b) in enumerate(x_parts):
                sp.dma_start(x_sb[:, a:b, :], x_v[:, a:b, :]).then_inc(x_in[i], 16)
                if i == 0:
                    sp.dma_start(wq_sb[:, :, :], wq.rearrange("(o p) c -> p o c", p=P)).then_inc(wq_in, 16)
            sp.dma_start(wo_sb[:, :, :], wout.rearrange("(o p) c -> p o c", p=P)).then_inc(wo_in, 16)
            for i, w in enumerate((w_gate, w_up, w_down)):
                sp.dma_start(wf_sb[:, i, :].rearrange("p (a c) -> p a c", c=w.shape[1]),
                             w.rearrange("(a p) c -> p a c", p=P)).then_inc(wf_in[i], 16)
            for t in range(NT):
                sp.wait_ge(o_ready, t + 1)
                sp.dma_start(out_v[:, t, :], o_sb[:, t, :]).then_inc(out_done, 16)
            sp.wait_ge(out_done, 16 * NT)

        @block.gpsimd
        def _(pool):
            def done(ins):
                ins.then_inc(const_ready, 1)

            def diagonal(ap, base, cols):
                return nc.gpsimd.affine_select(out=ap, in_=ap, compare_op=ALU.not_equal, fill=1.0, base=base,
                                               pattern=[[-1, cols]], channel_multiplier=1)

            own = sem("pool_chain")
            n = [0]

            def link(ins):
                n[0] += 1
                ins.then_inc(own, 1)
                pool.wait_ge(own, n[0])

            link(nc.gpsimd.memset(ident[:, :], 0.0))
            done(diagonal(ident[:, :], 0, P))
            done(nc.gpsimd.memset(minus_half[:, :], -0.5))
            link(nc.gpsimd.memset(head_mask[:, :], 1.0))
            link(nc.gpsimd.affine_select(out=head_mask[:, :], in_=head_mask[:, :], compare_op=ALU.is_ge, fill=0.0,
                                         base=0, pattern=[[-HD, HH]], channel_multiplier=1))
            done(nc.gpsimd.affine_select(out=head_mask[:, :], in_=head_mask[:, :], compare_op=ALU.is_ge, fill=0.0,
                                         base=HD - 1, pattern=[[HD, HH]], channel_multiplier=-1))
            link(nc.gpsimd.memset(sel2[:, :], 0.0))
            link(diagonal(sel2[:, :], 0, P))
            done(diagonal(sel2[:, :], Q, P))
            link(nc.gpsimd.memset(causal[:, :], 0.0))
            done(nc.gpsimd.affine_select(out=causal[:, :], in_=causal[:, :], compare_op=ALU.is_ge, fill=NEG,
                                         base=0, pattern=[[-1, S]], channel_multiplier=1))
            link(nc.gpsimd.memset(ident_b[:, :], 0.0))
            done(diagonal(ident_b[:, :], 0, P))

            def power(i):
                pool.wait_ge(var_ready, i + 1)
                nc.gpsimd.tensor_tensor(rstd[:, i:i + 1], veps[:, i:i + 1], minus_half[:, :],
                                        ALU.pow).then_inc(rstd_ready, 1)

            def widen(c, part):
                pool.wait_ge(misc_read, misc_no[("k", c, HALVES - 1)] + 1)
                for hf, h in part:
                    nc.gpsimd.tensor_scalar(k_wide[:, hf, h, KT * c:KT * c + KT], kT[:, c, hf, :],
                                            head_mask[:, h:h + 1], 1.0, ALU.mult, ALU.mult).then_inc(kw_pool, 1)

            power(0)
            power(1)
            done(nc.gpsimd.memset(v_wide[:, :, :, :], 0.0))
            widen(0, KW_POOL)
            power(2)
            power(3)
            done(nc.gpsimd.memset(mean_w[:, :], 1.0 / WN))
            for s in range(SLOTS):
                u = s - 1
                if 0 <= u < NU:
                    pool.wait_ge(rden_ready, u + 1)
                    if u >= 3:
                        pool.wait_ge(tr_written, u - 2)
                    nc.gpsimd.tensor_tensor(p_norm[:, u % 3, :, 0:S], soft[:, u % 3, :, :],
                                            rden[:, u % 3, :, None].to_broadcast([P, HH, S]),
                                            ALU.mult).then_inc(pn_ready, 1)
                if s < 3:
                    power(4 + s)
                if 1 <= s <= 3:
                    widen(1, KW_POOL[2 * s - 2:2 * s])
                t, odd = divmod(s - OP0, 2)
                if 0 <= t < NT:
                    if not odd:
                        power(NT + t)
                    else:
                        pool.wait_ge(y_ready, t + 1)
                        if t >= 2:
                            pool.wait_ge(misc_written, misc_no[("xqT", t - 2)] + 1)
                        nc.gpsimd.tensor_scalar(y_int[:, t % 2, :], y_sb[:, t % 2, :], r_tok[:, 0, t:t + 1], MAGIC,
                                                ALU.mult, ALU.add).then_inc(yint_ready, 1)
                        pool.wait_ge(yint_ready, t + 1)
                        nc.gpsimd.tensor_scalar(xq_b[:, t % 2, :], y_int[:, t % 2, :], 1.0, -MAGIC,
                                                ALU.mult, ALU.add).then_inc(xq_ready, 1)
                for i in range(3 * NPIECE):
                    if s == TERN0 + i // 2:
                        pool.wait_ge(posneg_ready, i + 1)
                        w, c = divmod(i, NPIECE)
                        nc.gpsimd.tensor_tensor(tern[:, w, PIECE * c:PIECE * c + PIECE], pos[:, i % 2, :],
                                                neg[:, i % 2, :], ALU.subtract).then_inc(tern_ready, 1)
                t = s - GU0
                if 0 <= t < NT:
                    pool.wait_ge(r_ready, t + 1)
                    nc.gpsimd.tensor_scalar(h_int[:, t % 2, :], h_sb[:, t % 3, :], r_tok[:, 1, t:t + 1], MAGIC,
                                            ALU.mult, ALU.add).then_inc(hint_ready, 1)
                    pool.wait_ge(hint_ready, t + 1)
                    if t >= 2:
                        pool.wait_ge(tr_written, NU + t - 1)
                    nc.gpsimd.tensor_scalar(hq_b[:, t % 2, :], h_int[:, t % 2, :], 1.0, -MAGIC,
                                            ALU.mult, ALU.add).then_inc(hq_ready, 1)

        @block.scalar
        def _(act):
            act.dma_start(wkv_sb[:, :, :], wkv.rearrange("(o p) c -> p o c", p=P)).then_inc(wkv_in, 16)
            for par in range(2):
                act.dma_start(ctx_sb[S * par:S * par + S, :, :],
                              ctx_512[par:B:2, 0:S, :].rearrange("b k l -> k b l")).then_inc(ctx_in, 16)

            def copy(dst, src, scale=1.0, bias=0.0):
                return nc.scalar.activation(dst, src, ACT.Copy, scale=scale, bias=bias)

            def read_misc(job):
                n = misc_no[job]
                kind, i = job[0], job[1]
                bank = MI[n % 2]
                act.wait_ge(misc_written, n + 1)
                if kind == "wkvT":
                    last = copy(wkvT[:, :], bank[0:L, :])
                elif kind == "ctxT":
                    last = copy(ctxT[:, KT * i:KT * i + KT], bank[0:L, 0:KT])
                elif kind == "k":
                    last = copy(kT[:, i, job[2], :], bank[:, 0:KT])
                elif kind in ("wqT", "woT"):
                    last = copy((wqT if kind == "wqT" else woT)[:, :, :],
                                bank[:, :].rearrange("p (i o) -> p i o", i=HALVES))
                elif kind == "xT":
                    last = copy(xnT[:, :, P * i:P * i + P], bank[:, 0:C].rearrange("p (i o) -> p i o", i=HALVES))
                elif kind == "q":
                    last = copy(qT[:, :, 4 * i:4 * i + 4, 0:S],
                                bank[:, 0:2 * CT].rearrange("p (i b q) -> p i b q", i=HALVES, q=S), scale=SCALE)
                elif kind == "v":
                    const(act, "v_zero")
                    for par in range(2):
                        r = slice(Q * par, Q * par + Q)
                        last = copy(v_wide[r, VB * i:VB * i + VB, :, HD * par:HD * par + HD],
                                    bank[r, :].rearrange("p (b h d) -> p b h d", b=VB, d=HD))
                elif kind == "mean":
                    last = copy(w_scale[:, i:i + 1], bank[:, 0:1], bias=EPS)
                elif kind == "pv":
                    p, hf = divmod(i, HALVES)
                    last = copy(attnT[:, hf, 2 * S * p:2 * S * p + 2 * S], bank[:, 0:2 * S])
                elif kind == "wT":
                    k = job[2]
                    b16 = bank[:, :].bitcast(BF16)
                    if i < 2:
                        last = copy(wT[:, i, k, :], b16)
                    else:
                        last = copy(wdT[:, :, P * k:P * k + P], b16.rearrange("p (c o) -> p c o", o=P))
                elif kind == "xqT":
                    last = copy(xqT[:, i, :, :], bank[:, 0:P].bitcast(BF16).rearrange("p (i o) -> p i o", i=HALVES))
                last.then_inc(misc_read, 1)

            for job in misc[-1]:
                read_misc(job)
            for s in range(SLOTS):
                for job in misc[s]:
                    read_misc(job)
                u = s - LAG_T
                if 0 <= u < NU:
                    act.wait_ge(tr_written, u + 1)
                    if u >= 2:
                        act.wait_ge(misc_written, misc_no[("pv", u - 2)] + 1)
                    copy(pT[:, u % 2, :, :], TR[u % 2][:, :].rearrange("p (j q) -> p j q", j=HP)).then_inc(tr_read, 1)
                if s < NU:
                    act.wait_ge(sub_ready, s + 1)
                    nc.scalar.activation(soft[:, s % 3, :, :], soft[:, s % 3, :, :], ACT.Exp).then_inc(exp_ready, 1)
                w = s - ABS0
                if 0 <= w < 3:
                    act.wait_ge(wf_in[w], 16)
                    nc.scalar.activation(tern[:, w, :], wf_sb[:, w, :], ACT.Abs,
                                         accum_out=asum[:, w:w + 1]).then_inc(asum_ready, 1)
                t = s - GU0
                if 0 <= t < NT:
                    act.wait_ge(gu_scale_ready, t + 1)
                    for c in range(NG):
                        j = 4 * t + 2 * c
                        act.wait_ge(gu_written, j + 1)
                        if t >= 2:
                            act.wait_ge(h_ready, NG * (t - 2) + c + 1)
                        nc.scalar.activation(g_sb[:, t % 2, GC * c:GC * c + GC], SC[j % 3][:, :], ACT.Silu,
                                             scale=s_out[:, 0, t:t + 1]).then_inc(silu_ready, 1)
                t = s - HT0
                if 0 <= t < NT:
                    act.wait_ge(tr_written, NU + t + 1)
                    if t >= 2:
                        act.wait_ge(op_written, NT + t - 1)
                    n = NU + t
                    copy(hT[:, t % 2, :, :],
                         TR[n % 2][:, :].bitcast(BF16).rearrange("p (j q) -> p j q", j=NC8)).then_inc(tr_read, 1)

        @block.vector
        def _(dve):
            chain = [0]

            def link(ins):
                chain[0] += 1
                ins.then_inc(dve_chain, 1)
                dve.wait_ge(dve_chain, chain[0])

            nc.vector.memset(qT[:, :, :, S:], 0.0)
            nc.vector.memset(ctxT[:, T:], 0.0)
            nc.vector.memset(p_norm[:, :, :, S:], 0.0).then_inc(pads_ready, 1)

            def moments(i, t):
                link(nc.vector.bn_stats(stats[:, i, :], x_sb[:, t, :]))
                link(nc.vector.bn_aggr(mv[:, i, :], stats[:, i, :]))
                nc.vector.tensor_scalar(veps[:, i:i + 1], mv[:, i, 1:2], EPS, None, ALU.add).then_inc(var_ready, 1)

            def normalise(i, t, dst):
                dve.wait_ge(rstd_ready, i + 1)
                return nc.vector.tensor_scalar(dst, x_sb[:, t, :], mv[:, i, 0:1], rstd[:, i:i + 1],
                                               ALU.subtract, ALU.mult)

            def ln1_moments(t):
                dve.wait_ge(x_in[x_part(t)], 16)
                moments(t, t)

            def ln1(t):
                if t >= 4:
                    dve.wait_ge(misc_written, misc_no[("xT", t - 4)] + 1)
                normalise(t, t, xn_sb[:, t % 4, :]).then_inc(xn_ready, 1)

            def widen(c, part):
                const(dve, "head_mask")
                dve.wait_ge(misc_read, misc_no[("k", c, HALVES - 1)] + 1)
                for hf, h in part:
                    nc.vector.tensor_scalar(k_wide[:, hf, h, KT * c:KT * c + KT], kT[:, c, hf, :],
                                            head_mask[:, h:h + 1], None, ALU.mult).then_inc(kw_dve, 1)

            ln1_moments(0)
            ln1_moments(1)
            ln1(0)
            ln1(1)
            ln1_moments(2)
            ln1_moments(3)
            widen(0, KW_DVE)
            ln1(2)
            ln1(3)
            for s in range(SLOTS):
                u = s
                if u < NU:
                    sc = SC[u % 3][:, 0:HH * S].rearrange("p (h k) -> p h k", h=HH)
                    dve.wait_ge(scores_written, u + 1)
                    link(nc.vector.tensor_reduce(mx[:, u % 3, :], sc, axis=AX_X, op=ALU.max))
                    if u >= 3:
                        dve.wait_ge(pn_ready, u - 2)
                    nc.vector.tensor_tensor(soft[:, u % 3, :, :], sc, mx[:, u % 3, :, None].to_broadcast([P, HH, S]),
                                            ALU.subtract).then_inc(sub_ready, 1)
                u = s - 1
                if 0 <= u < NU:
                    dve.wait_ge(exp_ready, u + 1)
                    link(nc.vector.tensor_reduce(den[:, u % 3, :], soft[:, u % 3, :, :], axis=AX_X, op=ALU.add))
                    nc.vector.reciprocal(rden[:, u % 3, :], den[:, u % 3, :]).then_inc(rden_ready, 1)
                if s < 3:
                    ln1_moments(4 + s)
                    ln1(4 + s)
                if 1 <= s <= 5:
                    widen(1, KW_DVE[2 * s - 2:2 * s])
                t, odd = divmod(s - OP0, 2)
                if 0 <= t < NT:
                    if not odd:
                        dve.wait_ge(op_written, t + 1)
                        nc.vector.tensor_tensor(x_sb[:, t, :], OPB[:, 0:C], x_sb[:, t, :],
                                                ALU.add).then_inc(op_read, 1)
                        dve.wait_ge(op_read, t + 1)
                        moments(NT + t, t)
                    else:
                        if t >= 2:
                            dve.wait_ge(yint_ready, t - 1)
                        link(normalise(NT + t, t, y_sb[:, t % 2, :]))
                        link(nc.vector.tensor_reduce(amax[:, 0, t:t + 1], y_sb[:, t % 2, :], axis=AX_X, op=ALU.max,
                                                     apply_absolute_value=True))
                        link(nc.vector.tensor_scalar(s_tok[:, 0, t:t + 1], amax[:, 0, t:t + 1], 1.0 / 127.0, EPS,
                                                     ALU.mult, ALU.add))
                        nc.vector.reciprocal(r_tok[:, 0, t:t + 1], s_tok[:, 0, t:t + 1]).then_inc(y_ready, 1)
                        dve.wait_ge(misc_read, misc_no[("mean", 1)] + 1)
                        nc.vector.tensor_scalar(s_out[:, 0:2, t], w_scale[:, 0:2], s_tok[:, 0, t:t + 1], None,
                                                ALU.mult).then_inc(gu_scale_ready, 1)
                for i in range(3 * NPIECE):
                    if s == TERN0 + i // 2:
                        w, c = divmod(i, NPIECE)
                        if c == 0:
                            dve.wait_ge(misc_read, misc_no[("mean", w)] + 1)
                            link(nc.vector.tensor_scalar(w_thr[:, 0, w:w + 1], w_scale[:, w:w + 1], 0.5, None,
                                                         ALU.mult))
                            link(nc.vector.tensor_scalar(w_thr[:, 1, w:w + 1], w_scale[:, w:w + 1], -0.5, None,
                                                         ALU.mult))
                        if i >= 2:
                            dve.wait_ge(tern_ready, i - 1)
                        src = wf_sb[:, w, PIECE * c:PIECE * c + PIECE]
                        nc.vector.tensor_scalar(pos[:, i % 2, :], src, w_thr[:, 0, w:w + 1], None, ALU.is_gt)
                        nc.vector.tensor_scalar(neg[:, i % 2, :], src, w_thr[:, 1, w:w + 1], None,
                                                ALU.is_lt).then_inc(posneg_ready, 1)
                t = s - GU0
                if 0 <= t < NT:
                    for c in range(NG):
                        j = 4 * t + 2 * c + 1
                        cols = slice(GC * c, GC * c + GC)
                        dve.wait_ge(gu_written, j + 1)
                        dve.wait_ge(silu_ready, NG * t + c + 1)
                        if t >= 3 and c == 0:
                            dve.wait_ge(hint_ready, t - 2)
                        nc.vector.scalar_tensor_tensor(h_sb[:, t % 3, cols], SC[j % 3][:, :], s_out[:, 1, t:t + 1],
                                                       g_sb[:, t % 2, cols], ALU.mult, ALU.mult).then_inc(h_ready, 1)
                    dve.wait_ge(h_ready, NG * (t + 1))
                    link(nc.vector.tensor_reduce(amax[:, 1, t:t + 1], h_sb[:, t % 3, :], axis=AX_X, op=ALU.max,
                                                 apply_absolute_value=True))
                    link(nc.vector.tensor_scalar(s_tok[:, 1, t:t + 1], amax[:, 1, t:t + 1], 1.0 / 127.0, EPS,
                                                 ALU.mult, ALU.add))
                    nc.vector.tensor_tensor(s_out[:, 2, t:t + 1], s_tok[:, 1, t:t + 1], w_scale[:, 2:3], ALU.mult)
                    nc.vector.reciprocal(r_tok[:, 1, t:t + 1], s_tok[:, 1, t:t + 1]).then_inc(r_ready, 1)
                t = s - HT0
                if 0 <= t < NT:
                    dve.wait_ge(op_written, NT + t + 1)
                    nc.vector.scalar_tensor_tensor(o_sb[:, t, :], OPB[:, 0:C], s_out[:, 2, t:t + 1], x_sb[:, t, :],
                                                   ALU.mult, ALU.add).then_inc(o_ready, 1)

        @block.tensor
        def _(pe):
            def mm(*a, **k):
                return nc.tensor.matmul(*a, **k)

            def write_misc(job):
                n = misc_no[job]
                kind, i = job[0], job[1]
                bank = MI[n % 2]
                if n >= 2:
                    pe.wait_ge(misc_read, n - 1)
                if kind == "wkvT":
                    const(pe, "ident")
                    pe.wait_ge(wkv_in, 16)
                    for o in range(4):
                        last = nc.tensor.transpose(bank[0:L, P * o:P * o + P], wkv_sb[:, o, :], ident[:, :])
                elif kind == "ctxT":
                    pe.wait_ge(ctx_in, 32)
                    for j in range(4):
                        last = nc.tensor.transpose(bank[0:L, 2 * S * j:2 * S * j + 2 * S], ctx_sb[:, 4 * i + j, :],
                                                   ident[0:2 * S, 0:2 * S])
                elif kind == "k":
                    hf = job[2]
                    pe.wait_ge(misc_read, misc_no[("ctxT", i)] + 1)
                    last = mm(bank[:, 0:KT], wkvT[:, P * hf:P * hf + P], ctxT[:, KT * i:KT * i + KT],
                              start=True, stop=True)
                elif kind in ("wqT", "woT"):
                    pe.wait_ge(wq_in if kind == "wqT" else wo_in, 16)
                    w = wq_sb if kind == "wqT" else wo_sb
                    for a in range(HALVES):
                        for o in range(HALVES):
                            last = nc.tensor.transpose(bank[:, C * a + P * o:C * a + P * o + P],
                                                       w[:, o, P * a:P * a + P], ident[:, :])
                elif kind == "xT":
                    pe.wait_ge(xn_ready, i + 1)
                    for a in range(HALVES):
                        last = nc.tensor.transpose(bank[:, P * a:P * a + P], xn_sb[:, i % 4, P * a:P * a + P],
                                                   ident[:, :])
                elif kind == "q":
                    t = (CT * (i + 1) - 1) // P
                    pe.wait_ge(misc_read, misc_no[("xT", t)] + 1)
                    for o in range(HALVES):
                        for a in range(HALVES):
                            last = mm(bank[:, CT * o:CT * o + CT], wqT[:, a, P * o:P * o + P],
                                      xnT[:, a, CT * i:CT * i + CT], start=(a == 0), stop=(a == HALVES - 1))
                elif kind == "v":
                    if i == 0:
                        pe.wait_ge(pads_ready, 1)
                    pe.wait_ge(misc_read, misc_no[("ctxT", NKC - 1)] + 1)
                    wv = wkvT[:, C:2 * C].rearrange("l (h e d) -> l e h d", e=2, d=HD)
                    for b in range(VB):
                        c0 = S * (VB * i + b)
                        for par in range(2):
                            last = mm(bank[Q * par:Q * par + Q, P * b:P * b + P], ctxT[:, c0:c0 + Q], wv[:, par, :, :],
                                      start=True, stop=True)
                elif kind == "mean":
                    const(pe, "mean_w")
                    pe.wait_ge(asum_ready, i + 1)
                    last = mm(bank[:, 0:1], mean_w[:, :], asum[:, i:i + 1], start=True, stop=True)
                elif kind == "pv":
                    p, hf = divmod(i, HALVES)
                    pe.wait_ge(tr_read, i + 1)
                    pe.wait_ge(misc_read, misc_no[("v", 2 * p // VB)] + 1)
                    for par in range(2):
                        for j in range(HP):
                            last = mm(bank[32 * j:32 * j + 32, S * par:S * par + S],
                                      v_wide[:, 2 * p + par, HP * hf + j, :], pT[:, i % 2, j, Q * par:Q * par + S],
                                      start=True, stop=True)
                elif kind == "wT":
                    k = job[2]
                    pe.wait_ge(tern_ready, NPIECE * (i + 1))
                    const(pe, "ident_b")
                    b16 = bank[:, :].bitcast(BF16)
                    for c in range(NC8):
                        c0 = C * c + P * k if i < 2 else I * k + P * c
                        last = nc.tensor.transpose(b16[:, P * c:P * c + P], tern[:, i, c0:c0 + P], ident_b[:, :])
                elif kind == "xqT":
                    pe.wait_ge(xq_ready, i + 1)
                    b16 = bank[:, 0:P].bitcast(BF16)
                    for a in range(HALVES):
                        last = nc.tensor.transpose(b16[:, P * a:P * a + P], xq_b[:, i % 2, P * a:P * a + P],
                                                   ident_b[:, :])
                last.then_inc(misc_written, 1)

            def scores(u):
                p, hf = divmod(u, HALVES)
                bank = SC[u % 3]
                if u >= 3:
                    pe.wait_ge(sub_ready, u - 2)
                if u == 0:
                    const(pe, "causal")
                    pe.wait_ge(pads_ready, 1)
                if p % 2 == 0 and hf == 0:
                    pe.wait_ge(misc_read, misc_no[("q", p // 2)] + 1)
                if p % 4 == 0 and hf == 0:
                    pe.wait_ge(kw_dve, len(KW_DVE) * (p // 4 + 1))
                    pe.wait_ge(kw_pool, len(KW_POOL) * (p // 4 + 1))
                out_ = bank[:, 0:HH * S].rearrange("p (h k) -> p h k", h=HH)
                mm(out_, sel2[:, :], causal[:, None, :].to_broadcast([P, HH, S]), start=True, stop=False)
                for par in range(2):
                    c0 = S * (2 * p + par)
                    last = mm(out_[Q * par:Q * par + Q, :, :], qT[:, hf, 2 * p + par, :], k_wide[:, hf, :, c0:c0 + S],
                              start=False, stop=True)
                last.then_inc(scores_written, 1)

            def gate_up(t):
                for c in range(NG):
                    for w in range(2):
                        j = 4 * t + 2 * c + w
                        if j == 0:
                            pe.wait_ge(sub_ready, NU)
                            pe.wait_ge(misc_read, misc_no[("wT", 1, 1)] + 1)
                        if j >= 3:
                            pe.wait_ge((silu_ready, h_ready)[(j - 3) % 2], (j - 3) // 2 + 1)
                        if c == 0 and w == 0:
                            pe.wait_ge(misc_read, misc_no[("xqT", t)] + 1)
                        for a in range(HALVES):
                            last = mm(SC[j % 3][:, :], xqT[:, t, a, :], wT[:, w, a, GC * c:GC * c + GC],
                                      start=(a == 0), stop=(a == HALVES - 1))
                        last.then_inc(gu_written, 1)

            for job in misc[-1]:
                write_misc(job)
            for s in range(SLOTS):
                if s < NU:
                    scores(s)
                u = s - LAG_T
                if 0 <= u < NU:
                    pe.wait_ge(pn_ready, u + 1)
                    if u >= 2:
                        pe.wait_ge(tr_read, u - 1)
                    for j in range(HP):
                        last = nc.tensor.transpose(TR[u % 2][:, P * j:P * j + P],
                                                   p_norm[:, u % 3, 2 * j:2 * j + 2, :].rearrange("p h k -> p (h k)"),
                                                   ident[:, :])
                    last.then_inc(tr_written, 1)
                for job in misc[s]:
                    write_misc(job)
                t, odd = divmod(s - OP0, 2)
                if 0 <= t < NT and not odd:
                    need = (P * (t + 1) - 1) // (2 * S)
                    pe.wait_ge(misc_read, misc_no[("pv", HALVES * need + 1)] + 1)
                    pe.wait_ge(misc_read, misc_no[("woT", 0)] + 1)
                    if t >= 1:
                        pe.wait_ge(op_read, t)
                    for a in range(HALVES):
                        last = mm(OPB[:, 0:C], attnT[:, a, P * t:P * t + P], woT[:, a, :],
                                  start=(a == 0), stop=(a == HALVES - 1))
                    last.then_inc(op_written, 1)
                t = s - GU0
                if 0 <= t < NT:
                    gate_up(t)
                t = s - HT0
                if 0 <= t < NT:
                    n = NU + t
                    pe.wait_ge(hq_ready, t + 1)
                    pe.wait_ge(tr_read, n - 1)
                    b16 = TR[n % 2][:, :].bitcast(BF16)
                    for c in range(NC8):
                        last = nc.tensor.transpose(b16[:, P * c:P * c + P], hq_b[:, t % 2, P * c:P * c + P],
                                                   ident_b[:, :])
                    last.then_inc(tr_written, 1)
                    pe.wait_ge(tr_read, n + 1)
                    if t == 0:
                        pe.wait_ge(op_read, NT)
                        pe.wait_ge(misc_read, misc_no[("wT", 2, 1)] + 1)
                    else:
                        pe.wait_ge(o_ready, t)
                    for c in range(NC8):
                        last = mm(OPB[:, 0:C], hT[:, t % 2, c, :], wdT[:, c, :], start=(c == 0), stop=(c == NC8 - 1))
                    last.then_inc(op_written, 1)


_INS = ["x", "ctx_512", "L0_xattn_Wq", "L0_xattn_Wkv_expand", "L0_xattn_Wout",
        "L0_ffn_w_gate", "L0_ffn_w_up", "L0_ffn_w_down"]
_OUTS = [((16, 56, 256), "float32")]


def kernel(**inputs):
    import numpy as _np
    import concourse.bacc as _bacc
    from concourse import mybir as _mybir
    from concourse.bass_utils import run_bass_kernel_spmd as _run

    nc = _bacc.Bacc("TRN2", target_bir_lowering=False, num_devices=1)
    arrays, args = {}, []
    for name in _INS:
        a = _np.ascontiguousarray(inputs[name])
        arrays[f"in_{name}_dram"] = a
        args.append(nc.dram_tensor(f"in_{name}_dram", a.shape, _mybir.dt.from_np(a.dtype), kind="ExternalInput").ap())
    for i, (shape, dtype) in enumerate(_OUTS):
        dt = _mybir.dt.from_np(_np.dtype(dtype))
        args.append(nc.dram_tensor(f"out_{i}_dram", shape, dt, kind="ExternalOutput").ap())
    xattn_ffn(nc, *args)
    r = _run(nc, [arrays], core_ids=[0])
    return r.results[0]["out_0_dram"]
```

```python
from contextlib import ExitStack

import concourse.bass as bass
from concourse import mybir

F32, BF16 = mybir.dt.float32, mybir.dt.bfloat16
ALU = mybir.AluOpType
ACT = mybir.ActivationFunctionType
AX_X = mybir.AxisListType.X

P = 128
EPS = 1e-5
NEG = -3.0e38
MAGIC = 1.5 * 2.0 ** 23


PLAN = {'lag_t': 3,
 'lag_v': 4,
 'op0': 8,
 'y0': 9,
 'xt0': 11,
 'gu0': 18,
 'ht_lag': 2,
 'dn_lag': 0,
 'abs0': 7,
 'mean0': 9,
 'tern0': 7,
 'wt0': 18,
 'misc': [(('wkvT', 0), -1), (('xT', 0), -1), (('ctxT', 0), -1), (('k', 0, 0), -1), (('k', 0, 1), -1), (('xT', 3), 1),
          (('wqT', 0), -1), (('xT', 1), -1), (('q', 0), -1), (('k', 1, 0), 1), (('v', 1), 8), (('xT', 2), 2),
          (('k', 1, 1), 2), (('v', 0), 4), (('q', 2), 5), (('woT', 0), 4), (('xT', 5), 3), (('q', 1), 3),
          (('xT', 4), 3), (('xT', 6), 5), (('q', 3), 8), (('v', 2), 11), (('v', 3), 9), (('ctxT', 1), -1)],
 'kw': {(0, 0, 0): (-1, 'vector'),
        (0, 0, 1): (-1, 'vector'),
        (0, 0, 2): (-1, 'vector'),
        (0, 0, 3): (-1, 'vector'),
        (0, 0, 4): (-1, 'vector'),
        (0, 0, 5): (-1, 'gpsimd'),
        (0, 0, 6): (-1, 'gpsimd'),
        (0, 0, 7): (-1, 'gpsimd'),
        (0, 1, 0): (-1, 'vector'),
        (0, 1, 1): (-1, 'vector'),
        (0, 1, 2): (-1, 'gpsimd'),
        (0, 1, 3): (-1, 'vector'),
        (0, 1, 4): (-1, 'vector'),
        (0, 1, 5): (-1, 'gpsimd'),
        (0, 1, 6): (-1, 'vector'),
        (0, 1, 7): (-1, 'gpsimd'),
        (1, 0, 0): (3, 'vector'),
        (1, 0, 1): (2, 'gpsimd'),
        (1, 0, 2): (1, 'scalar'),
        (1, 0, 3): (1, 'vector'),
        (1, 0, 4): (2, 'vector'),
        (1, 0, 5): (2, 'gpsimd'),
        (1, 0, 6): (3, 'vector'),
        (1, 0, 7): (3, 'vector'),
        (1, 1, 0): (4, 'vector'),
        (1, 1, 1): (4, 'gpsimd'),
        (1, 1, 2): (5, 'vector'),
        (1, 1, 3): (5, 'vector'),
        (1, 1, 4): (2, 'scalar'),
        (1, 1, 5): (3, 'gpsimd'),
        (1, 1, 6): (3, 'vector'),
        (1, 1, 7): (4, 'vector')},
 'ln1': [0, 0, 2],
 'pool_order': ['norm', 'yn', 'ln1', 'widen', 'q', 'tern', 'hq', 'fin'],
 'act_order': ['exp', 'tr', 'misc', 'tern', 'silu', 'abs', 'widen', 'ht', 'fin'],
 'dve_order': ['ln1', 'sm', 'den', 'winv', 'widen', 'op', 'y', 'h', 'fin'],
 'pe_order': ['sc', 'tr', 'op', 'misc', 'gu', 'ht', 'dn'],
 'warm': 9,
 'sync_loads': ['x0', 'x1', 'wq0', 'x2', 'wo0', 'f0', 'f1', 'f2'],
 'act_loads': ['wkv0', 'ctx0', 'ctx1'],
 'x_parts': [(0, 2), (2, 4), (4, 7)],
 'quant': ['pool', 'pool', 'pool', 'pool', 'pool', 'pool', 'pool', 'pool', 'pool', 'pool', 'pool', 'pool', 'pool',
           'vector'],
 'wide': [1, 6],
 'fin': ['gpsimd', 'vector', 'vector', 'vector', 'gpsimd', 'vector', 'vector'],
 'sign_lag': 1}


def xattn_ffn(nc, x, ctx_512, wq, wkv, wout, w_gate, w_up, w_down, out):
    B, S, C = x.shape
    L = ctx_512.shape[2]
    I = w_gate.shape[0]
    HD = 16
    NH = C // HD
    T = B * S
    NT = T // P
    HALVES = C // P
    HH = NH // HALVES
    NP = B // 2
    NU = NP * HALVES
    Q = 64
    HP = HH // 2
    CT = 2 * 2 * S
    KT = 4 * 2 * S
    NQC, NKC = T // CT, T // KT
    VB = 4
    NV = B // VB
    NC8 = I // P
    GC = 512
    NG = I // GC
    HC = GC // P
    WN = I * C
    WF = WN // P
    PIECE = 1024
    NPIECE = WF // PIECE
    SCALE = float(HD) ** -0.5
    assert T % P == 0 and S <= Q and HALVES == 2 and NG == 2 and KT <= 512 and NT == 7

    LAG_T, LAG_V = PLAN["lag_t"], PLAN["lag_v"]
    OP0, Y0, XT0 = PLAN["op0"], PLAN["y0"], PLAN["xt0"]
    GU0 = PLAN["gu0"]
    HT0 = GU0 + PLAN["ht_lag"]
    DN_LAG = PLAN["dn_lag"]
    ABS0, MEAN0, TERN0, WT0 = PLAN["abs0"], PLAN["mean0"], PLAN["tern0"], PLAN["wt0"]
    WIDE = PLAN["wide"]
    QUANT = [lambda t: PLAN["quant"][2 * t], lambda t: PLAN["quant"][2 * t + 1]]
    SLOTS = HT0 + NT + DN_LAG
    ABS0 = 3
    MEAN0 = ABS0 + 2
    TERN0 = ABS0 + 3
    WT0 = TERN0 + 4

    misc = {s: [] for s in range(-1, SLOTS)}
    for job, s in PLAN["misc"]:
        misc[s].append(job)
    for w in range(3):
        misc[MEAN0 + w].append(("mean", w))
        for k in range(2):
            misc[WT0 + 2 * w + k].append(("wT", w, k))
    for u in range(NU):
        misc[u + LAG_V] += [("pv", u)]
    OP_AT = {OP0 + 2 * t: t for t in range(NT)}
    Y_AT = {Y0 + 2 * t: t for t in range(NT)}
    for t in range(NT):
        misc[XT0 + 2 * t] += [("xqT", t)]
    misc_no = {}
    for s in range(-1, SLOTS):
        for job in misc[s]:
            misc_no[job] = len(misc_no)

    def read(*jobs):
        return max(misc_no[j] for j in jobs) + 1

    with ExitStack() as ctx:
        def sb(name, shape, dt=F32):
            return ctx.enter_context(nc.sbuf_tensor(name, shape, dt))

        def sem(name):
            return ctx.enter_context(nc.semaphore(name))

        x_sb = sb("x_sb", [P, NT, C])
        ctx_sb = sb("ctx_sb", [2 * S, NP, L])
        wq_sb = sb("wq_sb", [P, HALVES, C])
        wkv_sb = sb("wkv_sb", [P, 4, L])
        wo_sb = sb("wo_sb", [P, HALVES, C])
        wf_sb = sb("wf_sb", [P, 3, WF])
        xn_sb = sb("xn_sb", [P, 4, C])
        xnT = sb("xnT", [P, HALVES, T])
        wqT = sb("wqT", [P, HALVES, C])
        woT = sb("woT", [P, HALVES, C])
        wkvT = sb("wkvT", [P, 2 * C])
        ctxT = sb("ctxT", [P, T + Q - S])
        kT = sb("kT", [P, NKC, HALVES, KT])
        k_wide = sb("k_wide", [P, HALVES, HH, T])
        qT = sb("qT", [P, HALVES, B, Q])
        warm = sb("warm", [P, 512], BF16)
        v_wide = sb("v_wide", [P, B, NH // 2, 2 * HD])
        soft = sb("soft", [P, 3, HH, S])
        p_norm = sb("p_norm", [P, 3, HH, Q])
        pT = sb("pT", [P, 2, HP, P])
        attnT = sb("attnT", [P, HALVES, T])
        mx = sb("mx", [P, 3, HH])
        den = sb("den", [P, 3, HH])
        rden = sb("rden", [P, 3, HH])
        ident = sb("ident", [P, P])
        ident_b = sb("ident_b", [P, P], BF16)
        sel2 = sb("sel2", [P, P], BF16)
        causal = sb("causal", [P, S], BF16)
        head_mask = sb("head_mask", [P, HH])
        parity_mask = sb("parity_mask", [P, 2])
        minus_half = sb("minus_half", [P, 2])
        minus_magic = sb("minus_magic", [P, 1])
        mean_w = sb("mean_w", [P, P])
        stats = sb("stats", [P, 2 * NT, 6])
        mv = sb("mv", [P, 2 * NT, 2])
        veps = sb("veps", [P, 2 * NT])
        negm = sb("negm", [P, 2 * NT])
        rstd = sb("rstd", [P, 2 * NT])
        y_sb = sb("y_sb", [P, 2, C])
        y_int = sb("y_int", [P, 2, C])
        xq_b = sb("xq_b", [P, 2, C], BF16)
        xqT = sb("xqT", [P, NT, HALVES, P], BF16)
        amax = sb("amax", [P, 2, NT])
        s_tok = sb("s_tok", [P, 2, NT])
        r_tok = sb("r_tok", [P, 2, NT])
        s_out = sb("s_out", [P, 3, NT])
        asum = sb("asum", [P, 3])
        w_scale = sb("w_scale", [P, 3])
        w_inv = sb("w_inv", [P, 3])
        tern = sb("tern", [P, 3, WF], BF16)
        wT = sb("wT", [P, 2, HALVES, I], BF16)
        wdT = sb("wdT", [P, NC8, C], BF16)
        kw = k_wide[:, :, :, :].rearrange("p a b c -> p (a b c)")
        g_sb = kw[:, 0:2 * I].rearrange("p (n i) -> p n i", n=2)
        h_sb = kw[:, 2 * I:5 * I].rearrange("p (n i) -> p n i", n=3)
        h_int = kw[:, 5 * I:7 * I].rearrange("p (n c i) -> p n c i", n=2, c=NG)
        hq_b = kw[:, 7 * I:8 * I].bitcast(BF16).rearrange("p (n c i) -> p n c i", n=2, c=NG)
        hT = kw[:, 8 * I:9 * I].bitcast(BF16).rearrange("p (n c t) -> p n c t", n=2, c=NC8)
        o_sb = kw[:, 9 * I:9 * I + NT * C].rearrange("p (t c) -> p t c", t=NT)

        banks = [ctx.enter_context(nc.psum_tensor(f"bank{i}", [P, 512], F32)) for i in range(8)]
        SC, TR, MI, OPB = banks[0:3], banks[3:5], banks[5:7], banks[7]

        x_parts = PLAN["x_parts"]
        x_in = [sem(f"x_in{i}") for i in range(len(x_parts))]
        ctx_in = [sem(f"ctx_in{i}") for i in range(NKC)]
        wkv_in, wq_in, wo_in = sem("wkv_in"), sem("wq_in"), sem("wo_in")
        wf_in = [sem(f"wf_in{i}") for i in range(3)]
        out_done = sem("out_done")
        const_ready = sem("const_ready")
        pads_ready = sem("pads_ready")
        dve_chain = sem("dve_chain")
        mv_ready = sem("mv_ready")
        yn_ready = sem("yn_ready")
        xn_ready = sem("xn_ready")
        kw_ready = {e: sem(f"kw_{e}") for e in ("vector", "gpsimd", "scalar")}
        misc_written, misc_read = sem("misc_written"), sem("misc_read")
        scores_written, sub_ready = sem("scores_written"), sem("sub_ready")
        exp_ready, rden_ready, pn_ready = sem("exp_ready"), sem("rden_ready"), sem("pn_ready")
        tr_written, tr_read = sem("tr_written"), sem("tr_read")
        op_written, op_read = sem("op_written"), sem("op_read")
        y_ready = sem("y_ready")
        yint_ready = sem("yint_ready")
        xq_ready = sem("xq_ready")
        asum_ready = sem("asum_ready")
        w_inv_ready = sem("w_inv_ready")
        w_int_ready, tern_ready = sem("w_int_ready"), sem("tern_ready")
        gu_written, silu_ready, h_ready = sem("gu_written"), sem("silu_ready"), sem("h_ready")
        gu_scale_ready = sem("gu_scale_ready")
        r_ready = sem("r_ready")
        hint_ready = {(e, c): sem(f"hint_{e}{c}") for e in ("pool", "vector") for c in range(NG)}
        hq_ready = {(e, c): sem(f"hq_{e}{c}") for e in ("pool", "vector") for c in range(NG)}

        def quantised(sems, t, c):
            e = QUANT[c](t)
            if t in WIDE:
                sems = hint_ready
            return sems[e, c], sum(QUANT[c](i) == e and (sems is hint_ready or i not in WIDE) for i in range(t + 1))
        o_ready = {e: sem(f"o_ready_{e}") for e in ("vector", "gpsimd")}
        dn_read = sem("dn_read")

        def finished(t):
            e = PLAN["fin"][t]
            return o_ready[e], PLAN["fin"][:t + 1].count(e)

        warm_ready = sem("warm_ready")

        CONSTS = ["ident", "minus_half", "head_mask", "sel2", "causal", "ident_b"]

        def const(eng, name):
            eng.wait_ge(const_ready, CONSTS.index(name) + 1)

        def x_part(t):
            return next(i for i, (a, b) in enumerate(x_parts) if a <= t < b)

        def widenings(engine, slot=None, upto=None):
            return [key for key, (at, e) in PLAN["kw"].items()
                    if e == engine and (slot is None or at == slot) and (upto is None or key[0] <= upto)]

        def widen(eng, engine, slot):
            for c, hf, h in widenings(engine, slot):
                dst, src = k_wide[:, hf, h, KT * c:KT * c + KT], kT[:, c, hf, :]
                const(eng, "head_mask")
                eng.wait_ge(misc_read, read(("k", c, hf)))
                if engine == "scalar":
                    ins = nc.scalar.activation(dst, src, ACT.Copy, scale=head_mask[:, h:h + 1])
                elif engine == "vector":
                    ins = nc.vector.tensor_scalar(dst, src, head_mask[:, h:h + 1], None, ALU.mult)
                else:
                    ins = nc.gpsimd.tensor_scalar(dst, src, head_mask[:, h:h + 1], 1.0, ALU.mult, ALU.mult)
                ins.then_inc(kw_ready[engine], 1)

        x_v = x.rearrange("b s c -> (b s) c").rearrange("(t p) c -> p t c", p=P)
        out_v = out.rearrange("b s c -> (b s) c").rearrange("(t p) c -> p t c", p=P)

        def quantise_half(eng, ops, t, c):
            e = QUANT[c](t)
            eng.wait_ge(r_ready, t + 1)
            if t >= 2:
                eng.wait_ge(*quantised(hq_ready, t - 2, c))
                if t - 2 in WIDE:
                    eng.wait_ge(tr_written, NU + NG * (t - 2) + c + 1)
            ops.tensor_scalar(h_int[:, t % 2, c, :], h_sb[:, t % 3, GC * c:GC * c + GC], r_tok[:, 1, t:t + 1], MAGIC,
                              ALU.mult, ALU.add).then_inc(hint_ready[e, c], 1)
            if t in WIDE:
                return
            eng.wait_ge(*quantised(hint_ready, t, c))
            if t >= 2:
                eng.wait_ge(tr_written, NU + NG * (t - 2) + c + 1)
            ops.tensor_scalar(hq_b[:, t % 2, c, :], h_int[:, t % 2, c, :], 1.0, -MAGIC,
                              ALU.mult, ALU.add).then_inc(hq_ready[e, c], 1)

        block = ctx.enter_context(nc.Block())

        def load(eng, name):
            kind, i = name[:-1], int(name[-1])
            if kind == "x":
                a, b = x_parts[i]
                eng.dma_start(x_sb[:, a:b, :], x_v[:, a:b, :]).then_inc(x_in[i], 16)
            elif kind == "ctx":
                for par in range(2):
                    eng.dma_start(ctx_sb[S * par:S * par + S, 4 * i:4 * i + 4, :],
                                  ctx_512[8 * i + par:8 * i + 8:2, 0:S, :].rearrange("b k l -> k b l")
                                  ).then_inc(ctx_in[i], 16)
            elif kind == "wkv":
                eng.dma_start(wkv_sb[:, :, :], wkv.rearrange("(o p) c -> p o c", p=P)).then_inc(wkv_in, 16)
            elif kind == "wq":
                eng.dma_start(wq_sb[:, :, :], wq.rearrange("(o p) c -> p o c", p=P)).then_inc(wq_in, 16)
            elif kind == "wo":
                eng.dma_start(wo_sb[:, :, :], wout.rearrange("(o p) c -> p o c", p=P)).then_inc(wo_in, 16)
            else:
                w = (w_gate, w_up, w_down)[i]
                eng.dma_start(wf_sb[:, i, :].rearrange("p (a c) -> p a c", c=w.shape[1]),
                              w.rearrange("(a p) c -> p a c", p=P)).then_inc(wf_in[i], 16)

        @block.sync
        def _(sp):
            for name in PLAN["sync_loads"]:
                load(sp, name)
            for t in range(NT):
                sp.wait_ge(*finished(t))
                sp.dma_start(out_v[:, t, :], o_sb[:, t, :]).then_inc(out_done, 16)
            sp.wait_ge(out_done, 16 * NT)

        @block.gpsimd
        def _(pool):
            def done(ins):
                ins.then_inc(const_ready, 1)

            def diagonal(ap, base, cols):
                return nc.gpsimd.affine_select(out=ap, in_=ap, compare_op=ALU.not_equal, fill=1.0, base=base,
                                               pattern=[[-1, cols]], channel_multiplier=1)

            own = sem("pool_chain")
            n = [0]

            def link(ins):
                n[0] += 1
                ins.then_inc(own, 1)
                pool.wait_ge(own, n[0])

            link(nc.gpsimd.memset(ident[:, :], 0.0))
            done(diagonal(ident[:, :], 0, P))
            done(nc.gpsimd.memset(minus_half[:, :], -0.5))
            link(nc.gpsimd.memset(head_mask[:, :], 1.0))
            link(nc.gpsimd.affine_select(out=head_mask[:, :], in_=head_mask[:, :], compare_op=ALU.is_ge, fill=0.0,
                                         base=0, pattern=[[-HD, HH]], channel_multiplier=1))
            done(nc.gpsimd.affine_select(out=head_mask[:, :], in_=head_mask[:, :], compare_op=ALU.is_ge, fill=0.0,
                                         base=HD - 1, pattern=[[HD, HH]], channel_multiplier=-1))
            link(nc.gpsimd.memset(sel2[:, :], 0.0))
            link(diagonal(sel2[:, :], 0, P))
            done(diagonal(sel2[:, :], Q, P))
            link(nc.gpsimd.memset(causal[:, :], 0.0))
            done(nc.gpsimd.affine_select(out=causal[:, :], in_=causal[:, :], compare_op=ALU.is_ge, fill=NEG,
                                         base=0, pattern=[[-1, S]], channel_multiplier=1))
            link(nc.gpsimd.memset(ident_b[:, :], 0.0))
            done(diagonal(ident_b[:, :], 0, P))

            def power(i, n=1):
                pool.wait_ge(mv_ready, i + n)
                link(nc.gpsimd.tensor_scalar(veps[:, i:i + n], mv[:, i:i + n, 1], 1.0, EPS, ALU.mult, ALU.add))
                nc.gpsimd.tensor_scalar(negm[:, i:i + n], mv[:, i:i + n, 0], -1.0, 1.0, ALU.mult, ALU.mult)
                link(nc.gpsimd.tensor_tensor(rstd[:, i:i + n], veps[:, i:i + n], minus_half[:, 0:n], ALU.pow))

            def normalise(i, t, dst, ready):
                nc.gpsimd.tensor_scalar(dst, x_sb[:, t, :], negm[:, i:i + 1], rstd[:, i:i + 1],
                                        ALU.add, ALU.mult).then_inc(ready, 1)

            def ln1(t):
                if t >= 4:
                    pool.wait_ge(misc_written, misc_no[("xT", t - 4)] + 1)
                normalise(t, t, xn_sb[:, t % 4, :], xn_ready)

            for t in range(0, 4, 2):
                power(t, 2)
                ln1(t)
                ln1(t + 1)
            widen(pool, "gpsimd", -1)
            steps = {}

            def step(s):
                u = s - 1
                if 0 <= u < NU:
                    pool.wait_ge(rden_ready, u + 1)
                    if u >= 3:
                        pool.wait_ge(tr_written, u - 2)
                    nc.gpsimd.tensor_tensor(p_norm[:, u % 3, :, 0:S], soft[:, u % 3, :, :],
                                            rden[:, u % 3, :, None].to_broadcast([P, HH, S]),
                                            ALU.mult).then_inc(pn_ready, 1)
            steps["norm"] = step

            def step(s):
                for i, at in enumerate(PLAN["ln1"]):
                    if s == at:
                        power(4 + i)
                        ln1(4 + i)
            steps["ln1"] = step

            def step(s):
                widen(pool, "gpsimd", s)
            steps["widen"] = step

            def step(s):
                if s in OP_AT:
                    t = OP_AT[s]
                    if t >= 2:
                        pool.wait_ge(yint_ready, t - 1)
                    power(NT + t)
                    normalise(NT + t, t, y_sb[:, t % 2, :], yn_ready)
            steps["yn"] = step

            def step(s):
                if s in Y_AT:
                        t = Y_AT[s]
                        pool.wait_ge(y_ready, t + 1)
                        if t >= 2:
                            pool.wait_ge(misc_written, misc_no[("xqT", t - 2)] + 1)
                        nc.gpsimd.tensor_scalar(y_int[:, t % 2, :], y_sb[:, t % 2, :], r_tok[:, 0, t:t + 1], MAGIC,
                                                ALU.mult, ALU.add).then_inc(yint_ready, 1)
                        pool.wait_ge(yint_ready, t + 1)
                        nc.gpsimd.tensor_scalar(xq_b[:, t % 2, :], y_int[:, t % 2, :], 1.0, -MAGIC,
                                                ALU.mult, ALU.add).then_inc(xq_ready, 1)
            steps["q"] = step

            def step(s):
                for i in range(3 * NPIECE):
                    if s == TERN0 + i:
                        w, c = divmod(i, NPIECE)
                        pool.wait_ge(w_inv_ready, w + 1)
                        piece = wf_sb[:, w, PIECE * c:PIECE * c + PIECE]
                        nc.gpsimd.tensor_scalar(piece, piece, w_inv[:, w:w + 1], MAGIC, ALU.mult,
                                                ALU.add).then_inc(w_int_ready, 1)
            steps["tern"] = step

            def step(s):
                t = s - GU0
                if 0 <= t < NT:
                    for c in range(NG):
                        if QUANT[c](t) == "pool":
                            quantise_half(pool, nc.gpsimd, t, c)
            steps["hq"] = step

            def step(s):
                t = s - HT0 - DN_LAG
                if 0 <= t < NT and PLAN["fin"][t] != "vector":
                    pool.wait_ge(dn_read, PLAN["fin"][:t + 1].count("gpsimd"))
                    nc.gpsimd.tensor_tensor(o_sb[:, t, :], o_sb[:, t, :], x_sb[:, t, :],
                                            ALU.add).then_inc(o_ready["gpsimd"], 1)
            steps["fin"] = step

            for s in range(SLOTS):
                for step_name in PLAN["pool_order"]:
                    steps[step_name](s)

        @block.scalar
        def _(act):
            for name in PLAN["act_loads"]:
                load(act, name)

            def copy(dst, src, scale=1.0, bias=0.0):
                return nc.scalar.activation(dst, src, ACT.Copy, scale=scale, bias=bias)

            def read_misc(job):
                n = misc_no[job]
                kind, i = job[0], job[1]
                bank = MI[n % 2]
                act.wait_ge(misc_written, n + 1)
                if kind == "wkvT":
                    last = copy(wkvT[0:L, :], bank[0:L, :])
                elif kind == "ctxT":
                    last = copy(ctxT[0:L, KT * i:KT * i + KT], bank[0:L, 0:KT])
                elif kind == "k":
                    last = copy(kT[:, i, job[2], :], bank[:, 0:KT])
                elif kind in ("wqT", "woT"):
                    last = copy((wqT if kind == "wqT" else woT)[:, :, :],
                                bank[:, :].rearrange("p (i o) -> p i o", i=HALVES))
                elif kind == "xT":
                    last = copy(xnT[:, :, P * i:P * i + P], bank[:, 0:C].rearrange("p (i o) -> p i o", i=HALVES))
                elif kind == "q":
                    last = copy(qT[:, :, 4 * i:4 * i + 4, 0:S],
                                bank[:, 0:2 * CT].rearrange("p (i b q) -> p i b q", i=HALVES, q=S), scale=SCALE)
                elif kind == "v":
                    act.wait_ge(pads_ready, 1)
                    for par in range(2):
                        last = copy(v_wide[:, VB * i:VB * i + VB, :, HD * par:HD * par + HD],
                                    bank[:, :].rearrange("p (b h d) -> p b h d", b=VB, d=HD),
                                    scale=parity_mask[:, par:par + 1])
                elif kind == "mean":
                    last = copy(w_scale[:, i:i + 1], bank[:, 0:1], bias=EPS)
                elif kind == "pv":
                    p, hf = divmod(i, HALVES)
                    last = copy(attnT[:, hf, 2 * S * p:2 * S * p + 2 * S], bank[:, 0:2 * S])
                elif kind == "wT":
                    k = job[2]
                    b16 = bank[:, :].bitcast(BF16)
                    if i < 2:
                        last = copy(wT[:, i, k, :], b16)
                    else:
                        last = copy(wdT[:, :, P * k:P * k + P], b16.rearrange("p (c o) -> p c o", o=P))
                elif kind == "xqT":
                    last = copy(xqT[:, i, :, :], bank[:, 0:P].bitcast(BF16).rearrange("p (i o) -> p i o", i=HALVES))
                last.then_inc(misc_read, 1)

            for job in misc[-1]:
                read_misc(job)
            widen(act, "scalar", -1)
            steps = {}

            def step(s):
                u = s - 1
                if 0 <= u < NU:
                    act.wait_ge(sub_ready, u + 1)
                    nc.scalar.activation(soft[:, u % 3, :, :], soft[:, u % 3, :, :], ACT.Exp).then_inc(exp_ready, 1)
            steps["exp"] = step

            def step(s):
                for job in misc[s]:
                    read_misc(job)
            steps["misc"] = step

            def step(s):
                u = s - LAG_T
                if 0 <= u < NU:
                    act.wait_ge(tr_written, u + 1)
                    if u >= 2:
                        act.wait_ge(misc_written, misc_no[("pv", u - 2)] + 1)
                    copy(pT[:, u % 2, :, :], TR[u % 2][:, :].rearrange("p (j q) -> p j q", j=HP)).then_inc(tr_read, 1)
            steps["tr"] = step

            def step(s):
                widen(act, "scalar", s)
            steps["widen"] = step

            def step(s):
                w = s - ABS0
                if 0 <= w < 3:
                    act.wait_ge(wf_in[w], 16)
                    nc.scalar.activation(tern[:, w, :], wf_sb[:, w, :], ACT.Abs,
                                         accum_out=asum[:, w:w + 1]).then_inc(asum_ready, 1)
            steps["abs"] = step

            def step(s):
                for i in range(3 * NPIECE):
                    if s == TERN0 + i + PLAN["sign_lag"]:
                        act.wait_ge(w_int_ready, i + 1)
                        w, c = divmod(i, NPIECE)
                        cols = slice(PIECE * c, PIECE * c + PIECE)
                        nc.scalar.activation(tern[:, w, cols], wf_sb[:, w, cols], ACT.Sign,
                                             bias=minus_magic[:, :]).then_inc(tern_ready, 1)
            steps["tern"] = step

            def step(s):
                t = s - GU0
                if 0 <= t < NT:
                    act.wait_ge(gu_scale_ready, t + 1)
                    for c in range(NG):
                        j = 4 * t + 2 * c
                        act.wait_ge(gu_written, j + 1)
                        if t >= 2:
                            act.wait_ge(h_ready, NG * (t - 2) + c + 1)
                        nc.scalar.activation(g_sb[:, t % 2, GC * c:GC * c + GC], SC[j % 3][:, :], ACT.Silu,
                                             scale=s_out[:, 0, t:t + 1]).then_inc(silu_ready, 1)
            steps["silu"] = step

            def step(s):
                t = s - HT0
                if 0 <= t < NT:
                    for c in range(NG):
                        n = NU + NG * t + c
                        act.wait_ge(tr_written, n + 1)
                        if t >= 2 and c == 0:
                            act.wait_ge(op_written, NT + t - 1)
                        dst = hT[:, t % 2, HC * c:HC * c + HC, :]
                        if t in WIDE:
                            copy(dst, TR[n % 2][:, 0:GC].rearrange("p (j q) -> p j q", j=HC),
                                 bias=-MAGIC).then_inc(tr_read, 1)
                        else:
                            copy(dst, TR[n % 2][:, 0:GC // 2].bitcast(BF16).rearrange("p (j q) -> p j q", j=HC)
                                 ).then_inc(tr_read, 1)
            steps["ht"] = step

            def step(s):
                t = s - HT0 - DN_LAG
                if 0 <= t < NT and PLAN["fin"][t] != "vector":
                    act.wait_ge(op_written, NT + t + 1)
                    nc.scalar.activation(o_sb[:, t, :], OPB[:, 0:C], ACT.Copy,
                                         scale=s_out[:, 2, t:t + 1]).then_inc(dn_read, 1)
            steps["fin"] = step

            for s in range(SLOTS):
                for step_name in PLAN["act_order"]:
                    steps[step_name](s)

        @block.vector
        def _(dve):
            chain = [0]

            def link(ins):
                chain[0] += 1
                ins.then_inc(dve_chain, 1)
                dve.wait_ge(dve_chain, chain[0])

            nc.vector.memset(warm[:, :], 0.0).then_inc(warm_ready, 1)
            nc.vector.memset(wkvT[L:, :], 0.0)
            for par in range(2):
                for half in range(2):
                    nc.vector.memset(parity_mask[Q * half:Q * half + Q, par:par + 1], float(par == half))
            nc.vector.memset(ctxT[L:, :], 0.0)
            nc.vector.memset(minus_magic[:, :], -MAGIC)
            nc.vector.memset(qT[:, :, :, S:], 0.0)
            nc.vector.memset(ctxT[0:L, T:], 0.0)
            nc.vector.memset(p_norm[:, :, :, S:], 0.0).then_inc(pads_ready, 1)

            def moments(i, t):
                link(nc.vector.bn_stats(stats[:, i, :], x_sb[:, t, :]))
                nc.vector.bn_aggr(mv[:, i, :], stats[:, i, :]).then_inc(mv_ready, 1)

            def ln1_moments(t):
                dve.wait_ge(x_in[x_part(t)], 16)
                moments(t, t)

            for t in range(4):
                ln1_moments(t)
            nc.vector.memset(mean_w[:, :], 1.0 / WN).then_inc(pads_ready, 1)
            widen(dve, "vector", -1)
            steps = {}

            def step(s):
                u = s
                if u < NU:
                    sc = SC[u % 3][:, 0:HH * S].rearrange("p (h k) -> p h k", h=HH)
                    dve.wait_ge(scores_written, u + 1)
                    link(nc.vector.tensor_reduce(mx[:, u % 3, :], sc, axis=AX_X, op=ALU.max))
                    if u >= 3:
                        dve.wait_ge(pn_ready, u - 2)
                    nc.vector.tensor_tensor(soft[:, u % 3, :, :], sc, mx[:, u % 3, :, None].to_broadcast([P, HH, S]),
                                            ALU.subtract).then_inc(sub_ready, 1)
            steps["sm"] = step

            def step(s):
                u = s - 1
                if 0 <= u < NU:
                    dve.wait_ge(exp_ready, u + 1)
                    link(nc.vector.tensor_reduce(den[:, u % 3, :], soft[:, u % 3, :, :], axis=AX_X, op=ALU.add))
                    nc.vector.reciprocal(rden[:, u % 3, :], den[:, u % 3, :]).then_inc(rden_ready, 1)
            steps["den"] = step

            def step(s):
                for i, at in enumerate(PLAN["ln1"]):
                    if s == at:
                        ln1_moments(4 + i)
            steps["ln1"] = step

            def step(s):
                widen(dve, "vector", s)
            steps["widen"] = step

            def step(s):
                if s in OP_AT:
                        t = OP_AT[s]
                        dve.wait_ge(op_written, t + 1)
                        nc.vector.tensor_tensor(x_sb[:, t, :], OPB[:, 0:C], x_sb[:, t, :],
                                                ALU.add).then_inc(op_read, 1)
                        dve.wait_ge(op_read, t + 1)
                        moments(NT + t, t)
            steps["op"] = step

            def step(s):
                if s in Y_AT:
                        t = Y_AT[s]
                        dve.wait_ge(yn_ready, t + 1)
                        link(nc.vector.tensor_reduce(amax[:, 0, t:t + 1], y_sb[:, t % 2, :], axis=AX_X, op=ALU.max,
                                                     apply_absolute_value=True))
                        link(nc.vector.tensor_scalar(s_tok[:, 0, t:t + 1], amax[:, 0, t:t + 1], 1.0 / 127.0, EPS,
                                                     ALU.mult, ALU.add))
                        nc.vector.reciprocal(r_tok[:, 0, t:t + 1], s_tok[:, 0, t:t + 1]).then_inc(y_ready, 1)
                        dve.wait_ge(misc_read, misc_no[("mean", 1)] + 1)
                        nc.vector.tensor_scalar(s_out[:, 0:2, t], w_scale[:, 0:2], s_tok[:, 0, t:t + 1], None,
                                                ALU.mult).then_inc(gu_scale_ready, 1)
            steps["y"] = step

            def step(s):
                for w in range(3):
                    if s == MEAN0 + w:
                        dve.wait_ge(misc_read, misc_no[("mean", w)] + 1)
                        nc.vector.reciprocal(w_inv[:, w:w + 1], w_scale[:, w:w + 1]).then_inc(w_inv_ready, 1)
            steps["winv"] = step

            def step(s):
                t = s - GU0
                if 0 <= t < NT:
                    for c in range(NG):
                        j = 4 * t + 2 * c + 1
                        cols = slice(GC * c, GC * c + GC)
                        dve.wait_ge(gu_written, j + 1)
                        dve.wait_ge(silu_ready, NG * t + c + 1)
                        if t >= 3:
                            dve.wait_ge(*quantised(hint_ready, t - 3, c))
                        nc.vector.scalar_tensor_tensor(h_sb[:, t % 3, cols], SC[j % 3][:, :], s_out[:, 1, t:t + 1],
                                                       g_sb[:, t % 2, cols], ALU.mult, ALU.mult).then_inc(h_ready, 1)
                    dve.wait_ge(h_ready, NG * (t + 1))
                    link(nc.vector.tensor_reduce(amax[:, 1, t:t + 1], h_sb[:, t % 3, :], axis=AX_X, op=ALU.max,
                                                 apply_absolute_value=True))
                    link(nc.vector.tensor_scalar(s_tok[:, 1, t:t + 1], amax[:, 1, t:t + 1], 1.0 / 127.0, EPS,
                                                 ALU.mult, ALU.add))
                    nc.vector.tensor_tensor(s_out[:, 2, t:t + 1], s_tok[:, 1, t:t + 1], w_scale[:, 2:3], ALU.mult)
                    nc.vector.reciprocal(r_tok[:, 1, t:t + 1], s_tok[:, 1, t:t + 1]).then_inc(r_ready, 1)
                    for c in range(NG):
                        if QUANT[c](t) == "vector":
                            quantise_half(dve, nc.vector, t, c)
            steps["h"] = step

            def step(s):
                t = s - HT0 - DN_LAG
                if 0 <= t < NT:
                    if PLAN["fin"][t] != "vector":
                        return
                    dve.wait_ge(op_written, NT + t + 1)
                    nc.vector.scalar_tensor_tensor(o_sb[:, t, :], OPB[:, 0:C], s_out[:, 2, t:t + 1], x_sb[:, t, :],
                                                   ALU.mult, ALU.add).then_inc(o_ready["vector"], 1)
            steps["fin"] = step

            for s in range(SLOTS):
                for step_name in PLAN["dve_order"]:
                    steps[step_name](s)

        @block.tensor
        def _(pe):
            def mm(*a, **k):
                return nc.tensor.matmul(*a, **k)

            def write_misc(job):
                n = misc_no[job]
                kind, i = job[0], job[1]
                bank = MI[n % 2]
                if n >= 2:
                    pe.wait_ge(misc_read, n - 1)
                if kind == "wkvT":
                    const(pe, "ident")
                    pe.wait_ge(wkv_in, 16)
                    for o in range(4):
                        last = nc.tensor.transpose(bank[0:L, P * o:P * o + P], wkv_sb[:, o, :], ident[:, :])
                elif kind == "ctxT":
                    pe.wait_ge(ctx_in[i], 32)
                    for j in range(4):
                        last = nc.tensor.transpose(bank[0:L, 2 * S * j:2 * S * j + 2 * S], ctx_sb[:, 4 * i + j, :],
                                                   ident[0:2 * S, 0:2 * S])
                elif kind == "k":
                    hf = job[2]
                    pe.wait_ge(misc_read, read(("wkvT", 0), ("ctxT", i)))
                    pe.wait_ge(pads_ready, 1)
                    last = mm(bank[:, 0:KT], wkvT[:, P * hf:P * hf + P], ctxT[:, KT * i:KT * i + KT],
                              start=True, stop=True)
                elif kind in ("wqT", "woT"):
                    pe.wait_ge(wq_in if kind == "wqT" else wo_in, 16)
                    w = wq_sb if kind == "wqT" else wo_sb
                    for a in range(HALVES):
                        for o in range(HALVES):
                            last = nc.tensor.transpose(bank[:, C * a + P * o:C * a + P * o + P],
                                                       w[:, o, P * a:P * a + P], ident[:, :])
                elif kind == "xT":
                    pe.wait_ge(xn_ready, i + 1)
                    for a in range(HALVES):
                        last = nc.tensor.transpose(bank[:, P * a:P * a + P], xn_sb[:, i % 4, P * a:P * a + P],
                                                   ident[:, :])
                elif kind == "q":
                    t = (CT * (i + 1) - 1) // P
                    pe.wait_ge(misc_read, read(("wqT", 0), *[("xT", n) for n in range(t + 1)]))
                    for o in range(HALVES):
                        for a in range(HALVES):
                            last = mm(bank[:, CT * o:CT * o + CT], wqT[:, a, P * o:P * o + P],
                                      xnT[:, a, CT * i:CT * i + CT], start=(a == 0), stop=(a == HALVES - 1))
                elif kind == "v":
                    pe.wait_ge(misc_read, read(*[("ctxT", c) for c in range(NKC)]))
                    wv = wkvT[:, C:2 * C].rearrange("l (h e d) -> l e h d", e=2, d=HD)
                    for b in range(VB):
                        c0 = S * (VB * i + b)
                        for par in range(2):
                            last = mm(bank[Q * par:Q * par + Q, P * b:P * b + P], ctxT[:, c0:c0 + Q], wv[:, par, :, :],
                                      start=True, stop=True)
                elif kind == "mean":
                    pe.wait_ge(pads_ready, 2)
                    pe.wait_ge(asum_ready, i + 1)
                    last = mm(bank[:, 0:1], mean_w[:, :], asum[:, i:i + 1], start=True, stop=True)
                elif kind == "pv":
                    p, hf = divmod(i, HALVES)
                    pe.wait_ge(tr_read, i + 1)
                    pe.wait_ge(misc_read, misc_no[("v", 2 * p // VB)] + 1)
                    for par in range(2):
                        for j in range(HP):
                            last = mm(bank[32 * j:32 * j + 32, S * par:S * par + S],
                                      v_wide[:, 2 * p + par, HP * hf + j, :], pT[:, i % 2, j, Q * par:Q * par + S],
                                      start=True, stop=True)
                elif kind == "wT":
                    k = job[2]
                    pe.wait_ge(tern_ready, NPIECE * (i + 1))
                    const(pe, "ident_b")
                    b16 = bank[:, :].bitcast(BF16)
                    for c in range(NC8):
                        c0 = C * c + P * k if i < 2 else I * k + P * c
                        last = nc.tensor.transpose(b16[:, P * c:P * c + P], tern[:, i, c0:c0 + P], ident_b[:, :])
                elif kind == "xqT":
                    pe.wait_ge(xq_ready, i + 1)
                    b16 = bank[:, 0:P].bitcast(BF16)
                    for a in range(HALVES):
                        last = nc.tensor.transpose(b16[:, P * a:P * a + P], xq_b[:, i % 2, P * a:P * a + P],
                                                   ident_b[:, :])
                last.then_inc(misc_written, 1)

            def scores(u):
                p, hf = divmod(u, HALVES)
                bank = SC[u % 3]
                if u >= 3:
                    pe.wait_ge(sub_ready, u - 2)
                if u == 0:
                    const(pe, "causal")
                    pe.wait_ge(pads_ready, 1)
                if p % 2 == 0 and hf == 0:
                    pe.wait_ge(misc_read, read(("q", p // 2)))
                if p % 4 == 0 and hf == 0:
                    for e in kw_ready:
                        pe.wait_ge(kw_ready[e], len(widenings(e, upto=p // 4)))
                out_ = bank[:, 0:HH * S].rearrange("p (h k) -> p h k", h=HH)
                mm(out_, sel2[:, :], causal[:, None, :].to_broadcast([P, HH, S]), start=True, stop=False)
                for par in range(2):
                    c0 = S * (2 * p + par)
                    last = mm(out_[Q * par:Q * par + Q, :, :], qT[:, hf, 2 * p + par, :], k_wide[:, hf, :, c0:c0 + S],
                              start=False, stop=True)
                last.then_inc(scores_written, 1)

            def gate_up(t):
                for c in range(NG):
                    for w in range(2):
                        j = 4 * t + 2 * c + w
                        if j == 0:
                            pe.wait_ge(sub_ready, NU)
                            pe.wait_ge(misc_read, read(*[("wT", w, k) for w in range(2) for k in range(2)]))
                        if j >= 3:
                            pe.wait_ge((silu_ready, h_ready)[(j - 3) % 2], (j - 3) // 2 + 1)
                        if c == 0 and w == 0:
                            pe.wait_ge(misc_read, misc_no[("xqT", t)] + 1)
                        for a in range(HALVES):
                            last = mm(SC[j % 3][:, :], xqT[:, t, a, :], wT[:, w, a, GC * c:GC * c + GC],
                                      start=(a == 0), stop=(a == HALVES - 1))
                        last.then_inc(gu_written, 1)

            pe.wait_ge(warm_ready, 1)
            for _ in range(PLAN["warm"]):
                mm(OPB[:, :], warm[:, 0:P], warm[:, :], start=True, stop=True)
            for job in misc[-1]:
                write_misc(job)
            steps = {}

            def step(s):
                if s < NU:
                    scores(s)
            steps["sc"] = step

            def step(s):
                u = s - LAG_T
                if 0 <= u < NU:
                    pe.wait_ge(pn_ready, u + 1)
                    if u >= 2:
                        pe.wait_ge(tr_read, u - 1)
                    for j in range(HP):
                        last = nc.tensor.transpose(TR[u % 2][:, P * j:P * j + P],
                                                   p_norm[:, u % 3, 2 * j:2 * j + 2, :].rearrange("p h k -> p (h k)"),
                                                   ident[:, :])
                    last.then_inc(tr_written, 1)
            steps["tr"] = step

            def step(s):
                for job in misc[s]:
                    write_misc(job)
            steps["misc"] = step

            def step(s):
                if s in OP_AT:
                    t = OP_AT[s]
                    need = (P * (t + 1) - 1) // (2 * S)
                    pe.wait_ge(misc_read, read(("woT", 0), ("pv", HALVES * need + 1)))
                    if t >= 1:
                        pe.wait_ge(op_read, t)
                    for a in range(HALVES):
                        last = mm(OPB[:, 0:C], attnT[:, a, P * t:P * t + P], woT[:, a, :],
                                  start=(a == 0), stop=(a == HALVES - 1))
                    last.then_inc(op_written, 1)
            steps["op"] = step

            def step(s):
                t = s - GU0
                if 0 <= t < NT:
                    gate_up(t)
            steps["gu"] = step

            def step(s):
                t = s - HT0
                if 0 <= t < NT:
                    for h in range(NG):
                        n = NU + NG * t + h
                        pe.wait_ge(*quantised(hq_ready, t, h))
                        pe.wait_ge(tr_read, n - 1)
                        b16 = TR[n % 2][:, 0:GC // 2].bitcast(BF16)
                        for c in range(HC):
                            if t in WIDE:
                                last = nc.tensor.transpose(TR[n % 2][:, P * c:P * c + P],
                                                           h_int[:, t % 2, h, P * c:P * c + P], ident[:, :])
                            else:
                                last = nc.tensor.transpose(b16[:, P * c:P * c + P], hq_b[:, t % 2, h, P * c:P * c + P],
                                                           ident_b[:, :])
                        last.then_inc(tr_written, 1)
            steps["ht"] = step

            def step(s):
                t = s - HT0 - DN_LAG
                if 0 <= t < NT:
                    if t == 0:
                        pe.wait_ge(op_read, NT)
                        pe.wait_ge(misc_read, read(("wT", 2, 0), ("wT", 2, 1)))
                    else:
                        if PLAN["fin"][t - 1] == "vector":
                            pe.wait_ge(*finished(t - 1))
                        else:
                            pe.wait_ge(dn_read, PLAN["fin"][:t].count("gpsimd"))
                    for c in range(NC8):
                        if c % HC == 0:
                            pe.wait_ge(tr_read, NU + NG * t + c // HC + 1)
                        last = mm(OPB[:, 0:C], hT[:, t % 2, c, :], wdT[:, c, :], start=(c == 0), stop=(c == NC8 - 1))
                    last.then_inc(op_written, 1)
            steps["dn"] = step

            for s in range(SLOTS):
                for step_name in PLAN["pe_order"]:
                    steps[step_name](s)

_INS = ["x", "ctx_512", "L0_xattn_Wq", "L0_xattn_Wkv_expand", "L0_xattn_Wout",
        "L0_ffn_w_gate", "L0_ffn_w_up", "L0_ffn_w_down"]
_OUTS = [((16, 56, 256), "float32")]


def kernel(**inputs):
    import numpy as _np
    import concourse.bacc as _bacc
    from concourse import mybir as _mybir
    from concourse.bass_utils import run_bass_kernel_spmd as _run

    nc = _bacc.Bacc("TRN2", target_bir_lowering=False, num_devices=1)
    arrays, args = {}, []
    for name in _INS:
        a = _np.ascontiguousarray(inputs[name])
        arrays[f"in_{name}_dram"] = a
        args.append(nc.dram_tensor(f"in_{name}_dram", a.shape, _mybir.dt.from_np(a.dtype), kind="ExternalInput").ap())
    for i, (shape, dtype) in enumerate(_OUTS):
        dt = _mybir.dt.from_np(_np.dtype(dtype))
        args.append(nc.dram_tensor(f"out_{i}_dram", shape, dt, kind="ExternalOutput").ap())
    xattn_ffn(nc, *args)
    r = _run(nc, [arrays], core_ids=[0])
    return r.results[0]["out_0_dram"]
```

```python
from contextlib import ExitStack

from concourse import mybir

F32, BF16 = mybir.dt.float32, mybir.dt.bfloat16
ALU = mybir.AluOpType
ACT = mybir.ActivationFunctionType
AX_X = mybir.AxisListType.X

P = 128
EPS = 1e-5
NEG = -3.0e38
MAGIC = 1.5 * 2.0 ** 23


LAG_T, LAG_V = 3, 4
FFN_SLOT = 16
GU0 = 17
HT0 = GU0 + 2
DN0 = HT0 + 1
OP_SLOTS = [8, 10, 12, 14, 17, 18, 20]
Y_SLOTS = [10, 11, 13, 16, 18, 19, 21]
XQ_SLOTS = [13, 13, 15, 19, 20, 21, 23]
LN1_SLOTS = [0, 0, 1]
ABS_SLOTS = [3, 4, 6]
INVERSE_SLOTS = [7, 7, 9]
ROUND_SLOTS = [7, 7, 8, 8, 9, 10]
SIGN_SLOTS = [8, 9, 10, 11, 12, 13]
SILU_TABLES_SLOT = 16
WARM_PRODUCTS = 7
X_PARTS = [(0, 2), (2, 4), (4, 7)]
SYNC_LOADS = ['x0', 'ctx0', 'x1', 'ctx1', 'wq0', 'x2', 'f0', 'f2', 'wo0', 'f1']
ACT_LOADS = ['wkv0', 'tables']

MISC_JOBS = {-1: [('wkvT', 0), ('ctxT', 0), ('xT', 0), ('xT', 1), ('k', 0, 0), ('wqT', 0), ('k', 0, 1),
                  ('ctxT', 1), ('q', 0), ('k', 1, 0), ('xT', 3)],
             0: [('k', 1, 1)],
             2: [('xT', 2), ('v', 0), ('xT', 4), ('q', 1)],
             3: [('xT', 5)],
             4: [('woT', 0)],
             5: [('q', 2)],
             6: [('xT', 6), ('mean', 1)],
             7: [('mean', 0), ('v', 3)],
             8: [('v', 1), ('q', 3)],
             9: [('mean', 2)],
             10: [('wT', 0, 0)],
             11: [('wT', 0, 1), ('v', 2)],
             12: [('wT', 1, 0)],
             14: [('wT', 1, 1)],
             15: [('wT', 2, 1)],
             16: [('wT', 2, 0)]}
VECTOR_READS = [('mean', 1), ('pv', 0), ('pv', 12), ('pv', 13), ('pv', 3), ('pv', 9), ('wT', 0, 1), ('wT', 2, 0),
                ('woT', 0), ('xT', 1), ('xT', 2), ('xT', 4), ('xT', 6)]
WIDENINGS = {(-1, 'gpsimd'): [(0, 0, 5), (0, 0, 6), (0, 0, 7), (0, 1, 2), (0, 1, 4), (0, 1, 5), (1, 0, 3)],
             (-1, 'scalar'): [(0, 1, 6)],
             (-1, 'vector'): [(0, 0, 0), (0, 0, 1), (0, 0, 2), (0, 0, 3), (0, 0, 4), (0, 1, 0), (0, 1, 1),
                              (0, 1, 3), (0, 1, 7)],
             (1, 'scalar'): [(1, 0, 2), (1, 0, 6)],
             (2, 'gpsimd'): [(1, 0, 4), (1, 0, 5), (1, 1, 1)],
             (2, 'scalar'): [(1, 1, 7)],
             (2, 'vector'): [(1, 0, 0), (1, 0, 7), (1, 1, 2)],
             (3, 'vector'): [(1, 0, 1)],
             (4, 'vector'): [(1, 1, 3)],
             (5, 'gpsimd'): [(1, 1, 4), (1, 1, 5), (1, 1, 6)],
             (7, 'scalar'): [(1, 1, 0)]}
ROUNDER = [('gpsimd', 'gpsimd'), ('gpsimd', 'gpsimd'), ('gpsimd', 'gpsimd'), ('gpsimd', 'gpsimd'), ('gpsimd', 'gpsimd'),
           ('gpsimd', 'gpsimd'), ('vector', 'vector')]
FINISHER = ['gpsimd', 'gpsimd', 'vector', 'vector', 'gpsimd', 'vector', 'vector']


def xattn_ffn(nc, x, ctx_512, wq, wkv, wout, w_gate, w_up, w_down, out):
    B, S, C = x.shape
    L = ctx_512.shape[2]
    I = w_gate.shape[0]
    HD = 16
    R = 3
    NH = C // HD
    T = B * S
    NT = T // P
    HALVES = C // P
    HH = NH // HALVES
    NP = B // 2
    NU = NP * HALVES
    Q = 64
    HP = HH // 2
    CT = 2 * 2 * S
    KT = 4 * 2 * S
    NKC = T // KT
    VB = 4
    NC8 = I // P
    GC = 512
    NG = I // GC
    HC = GC // P
    WN = I * C
    WF = WN // P
    PIECE = 1024
    NPIECE = WF // PIECE
    SCALE = float(HD) ** -0.5
    assert T % P == 0 and S <= Q and HALVES == 2 and NG == 2 and KT <= 512 and NT == 7

    SLOTS = DN0 + NT

    OP_AT = {s: t for t, s in enumerate(OP_SLOTS)}
    Y_AT = {s: t for t, s in enumerate(Y_SLOTS)}
    for slots in (OP_SLOTS, Y_SLOTS, LN1_SLOTS, ABS_SLOTS, INVERSE_SLOTS, ROUND_SLOTS, SIGN_SLOTS):
        assert slots == sorted(slots)
    assert len(OP_AT) == len(Y_AT) == NT and LN1_SLOTS[-1] < OP_SLOTS[0] and SILU_TABLES_SLOT >= NU

    misc = {s: list(MISC_JOBS.get(s, [])) for s in range(-1, SLOTS)}
    for u in range(NU):
        misc[u + LAG_V] += [("pv", u)]
    for t in range(NT):
        misc[XQ_SLOTS[t]] += [("xqT", t)]
    misc_no = {job: n for n, job in enumerate(misc[-1])}
    for s in range(SLOTS):
        op_jobs = [("op", OP_AT[s])] if s in OP_AT else []
        dn_jobs = [("dn", s - DN0)] if 0 <= s - DN0 < NT else []
        for job in op_jobs + misc[s] + dn_jobs:
            misc_no[job] = len(misc_no)

    def reader(job):
        return "vector" if job in VECTOR_READS else "scalar"

    with ExitStack() as ctx:
        def sb(name, shape, dt=F32):
            return ctx.enter_context(nc.sbuf_tensor(name, shape, dt))

        def sem(name):
            return ctx.enter_context(nc.semaphore(name))

        x_sb = sb("x_sb", [P, NT, C])
        ctx_sb = sb("ctx_sb", [2 * S, NP, L])
        wq_sb = sb("wq_sb", [P, HALVES, C])
        wkv_sb = sb("wkv_sb", [P, 4, L])
        wo_sb = sb("wo_sb", [P, HALVES, C])
        wf_sb = sb("wf_sb", [P, 3, WF])
        xn_sb = sb("xn_sb", [P, 4, C])
        xnT = sb("xnT", [P, HALVES, T])
        wqT = sb("wqT", [P, HALVES, C])
        woT = sb("woT", [P, HALVES, C])
        wkvT = sb("wkvT", [P, 2 * C])
        ctxT = sb("ctxT", [P, T + Q - S])
        kT = sb("kT", [P, NKC, HALVES, KT])
        k_wide = sb("k_wide", [P, HALVES, HH, T])
        qT = sb("qT", [P, HALVES, B, Q])
        v_wide = sb("v_wide", [P, B, NH // 2, 2 * HD])
        soft = sb("soft", [P, R, HH, S])
        p_norm = sb("p_norm", [P, R, HH, Q])
        pT = sb("pT", [P, 2, HP, P])
        attnT = sb("attnT", [P, HALVES, T])
        mx = sb("mx", [P, R, HH])
        den = sb("den", [P, R, HH])
        rden = sb("rden", [P, R, HH])
        ident = sb("ident", [P, P])
        ident_b = sb("ident_b", [P, P], BF16)
        sel2 = sb("sel2", [P, P], BF16)
        causal = sb("causal", [P, S], BF16)
        head_mask = sb("head_mask", [P, HH])
        parity_mask = sb("parity_mask", [P, 2])
        minus_half = sb("minus_half", [P, 2])
        minus_magic = sb("minus_magic", [P, 1])
        table_in, table_out = sb("table_in", [P, 1]), sb("table_out", [P, 1])
        mean_w = sb("mean_w", [P, P])
        stats = sb("stats", [P, 2 * NT, 6])
        mv = sb("mv", [P, 2 * NT, 2])
        veps = sb("veps", [P, 2 * NT])
        negm = sb("negm", [P, 2 * NT])
        rstd = sb("rstd", [P, 2 * NT])
        y_sb = sb("y_sb", [P, 2, C])
        y_int = sb("y_int", [P, 2, C])
        xqT = sb("xqT", [P, NT, HALVES, P], BF16)
        amax = sb("amax", [P, 2, NT])
        s_tok = sb("s_tok", [P, 2, NT])
        r_tok = sb("r_tok", [P, 2, NT])
        s_out = sb("s_out", [P, 3, NT])
        asum = sb("asum", [P, 3])
        w_scale = sb("w_scale", [P, 3])
        w_inv = sb("w_inv", [P, 3])
        tern = sb("tern", [P, 3, WF], BF16)
        warm = tern[:, 0, 0:512]
        wT = sb("wT", [P, 2, HALVES, I], BF16)
        wdT = sb("wdT", [P, NC8, C], BF16)
        kw = k_wide[:, :, :, :].rearrange("p a b c -> p (a b c)")
        g_sb = kw[:, 0:2 * I].rearrange("p (n i) -> p n i", n=2)
        h_sb = kw[:, 2 * I:5 * I].rearrange("p (n i) -> p n i", n=3)
        h_int = kw[:, 5 * I:7 * I].rearrange("p (n c i) -> p n c i", n=2, c=NG)
        hT = kw[:, 7 * I:8 * I].bitcast(BF16).rearrange("p (n c t) -> p n c t", n=2, c=NC8)
        o_sb = kw[:, 8 * I:8 * I + NT * C].rearrange("p (t c) -> p t c", t=NT)

        banks = [ctx.enter_context(nc.psum_tensor(f"bank{i}", [P, 512], F32)) for i in range(8)]
        SC, TR, MI = banks[0:3], banks[3:5], banks[5:8]

        x_in = [sem(f"x_in{i}") for i in range(len(X_PARTS))]
        ctx_in = [sem(f"ctx_in{i}") for i in range(NKC)]
        wkv_in, wq_in, wo_in = sem("wkv_in"), sem("wq_in"), sem("wo_in")
        wf_in = [sem(f"wf_in{i}") for i in range(3)]
        out_done = sem("out_done")
        const_ready = sem("const_ready")
        pads_ready = sem("pads_ready")
        max_ready, den_ready, stats_ready = sem("max_ready"), sem("den_ready"), sem("stats_ready")
        y_amax_ready, y_scale_ready = sem("y_amax_ready"), sem("y_scale_ready")
        h_amax_ready, h_scale_ready = sem("h_amax_ready"), sem("h_scale_ready")
        dn_scale_ready = sem("dn_scale_ready")
        mv_ready = sem("mv_ready")
        xn_ready, yn_ready = sem("xn_ready"), sem("yn_ready")
        kw_ready = [[sem(f"kw_ready{c}{hf}") for hf in range(HALVES)] for c in range(NKC)]
        misc_written = sem("misc_written")
        misc_read = [sem(f"misc_read{i}") for i in range(3)]
        scores_written, sub_ready = sem("scores_written"), sem("sub_ready")
        exp_ready, rden_ready, pn_ready = sem("exp_ready"), sem("rden_ready"), sem("pn_ready")
        tr_written, tr_read = sem("tr_written"), sem("tr_read")
        veps_ready, negm_ready, rstd_ready = sem("veps_ready"), sem("negm_ready"), sem("rstd_ready")
        y_ready = sem("y_ready")
        yint_ready = sem("yint_ready")
        asum_ready = sem("asum_ready")
        w_inv_ready = sem("w_inv_ready")
        w_int_ready, tern_ready = sem("w_int_ready"), sem("tern_ready")
        gu_written, silu_ready, h_ready = sem("gu_written"), sem("silu_ready"), sem("h_ready")
        gu_scale_ready = sem("gu_scale_ready")
        table_in_ready = sem("table_in_ready")
        warm_ready = sem("warm_ready")
        o_ready = sem("o_ready")
        r_ready = sem("r_ready")
        hint_ready = {(e, c): sem(f"hint_{e}{c}") for e in ("gpsimd", "vector") for c in range(NG)}

        def rounded(t, c):
            e = ROUNDER[t][c]
            return hint_ready[e, c], sum(ROUNDER[i][c] == e for i in range(t + 1))

        def wait_read(eng, *jobs):
            for bank in range(3):
                counts = [misc_no[j] // 3 + 1 for j in jobs if misc_no[j] % 3 == bank]
                if counts:
                    eng.wait_ge(misc_read[bank], max(counts))

        def misc_read_at(job):
            return misc_read[misc_no[job] % 3], misc_no[job] // 3 + 1

        def finished(t):
            if FINISHER[t] == "vector":
                return misc_read_at(("dn", t))
            return o_ready, FINISHER[:t + 1].count("gpsimd")

        CONSTS = ["ident", "minus_half", "head_mask", "sel2", "causal", "ident_b"]

        def const(eng, name):
            eng.wait_ge(const_ready, CONSTS.index(name) + 1)

        def x_part(t):
            return next(i for i, (a, b) in enumerate(X_PARTS) if a <= t < b)

        def widen(eng, engine, slot):
            for c, hf, h in WIDENINGS.get((slot, engine), []):
                dst, src = k_wide[:, hf, h, KT * c:KT * c + KT], kT[:, c, hf, :]
                const(eng, "head_mask")
                wait_read(eng, ("k", c, hf))
                if engine == "scalar":
                    ins = nc.scalar.activation(dst, src, ACT.Copy, scale=head_mask[:, h:h + 1])
                elif engine == "vector":
                    ins = nc.vector.tensor_scalar(dst, src, head_mask[:, h:h + 1], None, ALU.mult)
                else:
                    ins = nc.gpsimd.tensor_scalar(dst, src, head_mask[:, h:h + 1], 1.0, ALU.mult, ALU.mult)
                ins.then_inc(kw_ready[c][hf], 1)

        x_v = x.rearrange("b s c -> (b s) c").rearrange("(t p) c -> p t c", p=P)
        out_v = out.rearrange("b s c -> (b s) c").rearrange("(t p) c -> p t c", p=P)

        def round_h(eng, ops, engine, t, c):
            if ROUNDER[t][c] != engine:
                return
            eng.wait_ge(r_ready, t + 1)
            if t >= 2:
                eng.wait_ge(tr_written, NU + NG * (t - 2) + c + 1)
            ops.tensor_scalar(h_int[:, t % 2, c, :], h_sb[:, t % 3, GC * c:GC * c + GC], r_tok[:, 1, t:t + 1], MAGIC,
                              ALU.mult, ALU.add).then_inc(hint_ready[engine, c], 1)

        block = ctx.enter_context(nc.Block())

        def load(eng, name):
            kind, i = name[:-1], int(name[-1])
            if kind == "x":
                a, b = X_PARTS[i]
                eng.dma_start(x_sb[:, a:b, :], x_v[:, a:b, :]).then_inc(x_in[i], 16)
            elif kind == "ctx":
                for par in range(2):
                    eng.dma_start(ctx_sb[S * par:S * par + S, 4 * i:4 * i + 4, :],
                                  ctx_512[8 * i + par:8 * i + 8:2, 0:S, :].rearrange("b k l -> k b l")
                                  ).then_inc(ctx_in[i], 16)
            elif kind == "wkv":
                eng.dma_start(wkv_sb[:, :, :], wkv.rearrange("(o p) c -> p o c", p=P)).then_inc(wkv_in, 16)
            elif kind == "wq":
                eng.dma_start(wq_sb[:, :, :], wq.rearrange("(o p) c -> p o c", p=P)).then_inc(wq_in, 16)
            elif kind == "wo":
                eng.dma_start(wo_sb[:, :, :], wout.rearrange("(o p) c -> p o c", p=P)).then_inc(wo_in, 16)
            else:
                w = (w_gate, w_up, w_down)[i]
                eng.dma_start(wf_sb[:, i, :].rearrange("p (a c) -> p a c", c=w.shape[1]),
                              w.rearrange("(a p) c -> p a c", p=P)).then_inc(wf_in[i], 16)

        def read_misc(eng, copy, job):
            n = misc_no[job]
            kind, i = job[0], job[1]
            bank = MI[n % 3]
            eng.wait_ge(misc_written, n + 1)
            if kind == "wkvT":
                last = copy(wkvT[0:L, :], bank[0:L, :])
            elif kind == "ctxT":
                last = copy(ctxT[0:L, KT * i:KT * i + KT], bank[0:L, 0:KT])
            elif kind == "k":
                last = copy(kT[:, i, job[2], :], bank[:, 0:KT])
            elif kind in ("wqT", "woT"):
                last = copy((wqT if kind == "wqT" else woT)[:, :, :],
                            bank[:, :].rearrange("p (i o) -> p i o", i=HALVES))
            elif kind == "xT":
                last = copy(xnT[:, :, P * i:P * i + P], bank[:, 0:C].rearrange("p (i o) -> p i o", i=HALVES))
            elif kind == "q":
                last = copy(qT[:, :, 4 * i:4 * i + 4, 0:S],
                            bank[:, 0:2 * CT].rearrange("p (i b q) -> p i b q", i=HALVES, q=S), scale=SCALE)
            elif kind == "v":
                eng.wait_ge(pads_ready, 1)
                for par in range(2):
                    last = copy(v_wide[:, VB * i:VB * i + VB, :, HD * par:HD * par + HD],
                                bank[:, :].rearrange("p (b h d) -> p b h d", b=VB, d=HD),
                                scale=parity_mask[:, par:par + 1])
            elif kind == "mean":
                last = copy(w_scale[:, i:i + 1], bank[:, 0:1], bias=EPS)
            elif kind == "pv":
                p, hf = divmod(i, HALVES)
                last = copy(attnT[:, hf, 2 * S * p:2 * S * p + 2 * S], bank[:, 0:2 * S])
            elif kind == "wT":
                k = job[2]
                b16 = bank[:, :].bitcast(BF16)
                if i < 2:
                    last = copy(wT[:, i, k, :], b16)
                else:
                    last = copy(wdT[:, :, P * k:P * k + P], b16.rearrange("p (c o) -> p c o", o=P))
            elif kind == "xqT":
                last = copy(xqT[:, i, :, :], bank[:, 0:C].rearrange("p (i o) -> p i o", i=HALVES), bias=-MAGIC)
            last.then_inc(misc_read[n % 3], 1)

        def read_misc_jobs(eng, copy, engine, s):
            for job in misc[s]:
                if reader(job) == engine:
                    read_misc(eng, copy, job)

        @block.sync
        def _(sp):
            for name in SYNC_LOADS:
                load(sp, name)
            for t in range(NT):
                sp.wait_ge(*finished(t))
                sp.dma_start(out_v[:, t, :], o_sb[:, t, :]).then_inc(out_done, 16)
            sp.wait_ge(out_done, 16 * NT)

        @block.gpsimd
        def _(pool):
            def done(ins):
                ins.then_inc(const_ready, 1)

            def diagonal(ap, base, cols):
                return nc.gpsimd.affine_select(out=ap, in_=ap, compare_op=ALU.not_equal, fill=1.0, base=base,
                                               pattern=[[-1, cols]], channel_multiplier=1)

            own = sem("pool_chain")
            n = [0]

            def link(ins):
                n[0] += 1
                ins.then_inc(own, 1)
                pool.wait_ge(own, n[0])

            link(nc.gpsimd.memset(ident[:, :], 0.0))
            done(diagonal(ident[:, :], 0, P))
            done(nc.gpsimd.memset(minus_half[:, :], -0.5))
            link(nc.gpsimd.memset(head_mask[:, :], 1.0))
            link(nc.gpsimd.affine_select(out=head_mask[:, :], in_=head_mask[:, :], compare_op=ALU.is_ge, fill=0.0,
                                         base=0, pattern=[[-HD, HH]], channel_multiplier=1))
            done(nc.gpsimd.affine_select(out=head_mask[:, :], in_=head_mask[:, :], compare_op=ALU.is_ge, fill=0.0,
                                         base=HD - 1, pattern=[[HD, HH]], channel_multiplier=-1))
            link(nc.gpsimd.memset(sel2[:, :], 0.0))
            link(diagonal(sel2[:, :], 0, P))
            done(diagonal(sel2[:, :], Q, P))
            link(nc.gpsimd.memset(causal[:, :], 0.0))
            done(nc.gpsimd.affine_select(out=causal[:, :], in_=causal[:, :], compare_op=ALU.is_ge, fill=NEG,
                                         base=0, pattern=[[-1, S]], channel_multiplier=1))
            link(nc.gpsimd.memset(ident_b[:, :], 0.0))
            done(diagonal(ident_b[:, :], 0, P))

            def moments_to_factors(i, n=1):
                pool.wait_ge(mv_ready, i + n)
                nc.gpsimd.tensor_scalar(veps[:, i:i + n], mv[:, i:i + n, 1], 1.0, EPS,
                                        ALU.mult, ALU.add).then_inc(veps_ready, n)
                nc.gpsimd.tensor_scalar(negm[:, i:i + n], mv[:, i:i + n, 0], -1.0, 1.0,
                                        ALU.mult, ALU.mult).then_inc(negm_ready, n)

            def power(i, n=1):
                pool.wait_ge(veps_ready, i + n)
                nc.gpsimd.tensor_tensor(rstd[:, i:i + n], veps[:, i:i + n], minus_half[:, 0:n],
                                        ALU.pow).then_inc(rstd_ready, n)

            def normalise(i, t, dst, ready):
                pool.wait_ge(negm_ready, i + 1)
                pool.wait_ge(rstd_ready, i + 1)
                nc.gpsimd.tensor_scalar(dst, x_sb[:, t, :], negm[:, i:i + 1], rstd[:, i:i + 1],
                                        ALU.add, ALU.mult).then_inc(ready, 1)

            def ln1(t):
                if t >= 4:
                    pool.wait_ge(misc_written, misc_no[("xT", t - 4)] + 1)
                normalise(t, t, xn_sb[:, t % 4, :], xn_ready)

            for t in range(0, 4, 2):
                moments_to_factors(t, 2)
                power(t, 2)
                ln1(t)
                ln1(t + 1)
            widen(pool, "gpsimd", -1)

            def normalise_probabilities(s):
                u = s - 1
                if 0 <= u < NU:
                    pool.wait_ge(rden_ready, u + 1)
                    if u >= R:
                        pool.wait_ge(tr_written, u - R + 1)
                    nc.gpsimd.tensor_tensor(p_norm[:, u % R, :, 0:S], soft[:, u % R, :, :],
                                            rden[:, u % R, :, None].to_broadcast([P, HH, S]),
                                            ALU.mult).then_inc(pn_ready, 1)

            def first_layer_norm(s):
                for i, at in enumerate(LN1_SLOTS):
                    if s == at:
                        moments_to_factors(4 + i)
                        power(4 + i)
                        ln1(4 + i)

            def widen_k(s):
                widen(pool, "gpsimd", s)

            def second_variance(s):
                if s in OP_AT:
                    moments_to_factors(NT + OP_AT[s])

            def second_rstd(s):
                if s in OP_AT:
                    power(NT + OP_AT[s])

            def second_layer_norm(s):
                if s in OP_AT:
                    t = OP_AT[s]
                    if t >= 2:
                        pool.wait_ge(y_amax_ready, t - 1)
                        pool.wait_ge(yint_ready, t - 1)
                    normalise(NT + t, t, y_sb[:, t % 2, :], yn_ready)

            def round_tokens(s):
                if s in Y_AT:
                    t = Y_AT[s]
                    pool.wait_ge(y_ready, t + 1)
                    if t >= 2:
                        pool.wait_ge(misc_written, misc_no[("xqT", t - 2)] + 1)
                    nc.gpsimd.tensor_scalar(y_int[:, t % 2, :], y_sb[:, t % 2, :], r_tok[:, 0, t:t + 1], MAGIC,
                                            ALU.mult, ALU.add).then_inc(yint_ready, 1)

            def round_weights(s):
                for i in range(3 * NPIECE):
                    if s == ROUND_SLOTS[i]:
                        w, c = divmod(i, NPIECE)
                        pool.wait_ge(w_inv_ready, w + 1)
                        piece = wf_sb[:, w, PIECE * c:PIECE * c + PIECE]
                        nc.gpsimd.tensor_scalar(piece, piece, w_inv[:, w:w + 1], MAGIC, ALU.mult,
                                                ALU.add).then_inc(w_int_ready, 1)

            def round_gated(s, c):
                t = s - GU0
                if 0 <= t < NT:
                    round_h(pool, nc.gpsimd, "gpsimd", t, c)

            def add_residual(s):
                t = s - DN0
                if 0 <= t < NT and FINISHER[t] != "vector":
                    wait_read(pool, ("dn", t))
                    nc.gpsimd.tensor_tensor(o_sb[:, t, :], o_sb[:, t, :], x_sb[:, t, :],
                                            ALU.add).then_inc(o_ready, 1)

            for s in range(FFN_SLOT):
                normalise_probabilities(s)
                second_variance(s)
                second_rstd(s)
                first_layer_norm(s)
                second_layer_norm(s)
                round_tokens(s)
                round_weights(s)
                widen_k(s)
            for s in range(FFN_SLOT, SLOTS):
                second_variance(s)
                second_rstd(s)
                round_tokens(s)
                round_gated(s, 0)
                round_gated(s, 1)
                normalise_probabilities(s)
                second_layer_norm(s)
                add_residual(s)

        @block.scalar
        def _(act):
            def load_tables(function):
                nc.scalar.activation(table_out[:, :], table_in[:, :], function)

            for name in ACT_LOADS:
                if name == "tables":
                    act.wait_ge(table_in_ready, 1)
                    load_tables(ACT.Exp)
                else:
                    load(act, name)

            def copy(dst, src, scale=1.0, bias=0.0):
                return nc.scalar.activation(dst, src, ACT.Copy, scale=scale, bias=bias)

            read_misc_jobs(act, copy, "scalar", -1)
            widen(act, "scalar", -1)

            def exponentials(s):
                u = s - 1
                if 0 <= u < NU:
                    act.wait_ge(sub_ready, u + 1)
                    nc.scalar.activation(soft[:, u % R, :, :], soft[:, u % R, :, :], ACT.Exp).then_inc(exp_ready, 1)

            def load_silu_tables(s):
                if s == SILU_TABLES_SLOT:
                    load_tables(ACT.Silu)

            def read_misc_banks(s):
                read_misc_jobs(act, copy, "scalar", s)

            def read_probabilities(s):
                u = s - LAG_T
                if 0 <= u < NU:
                    act.wait_ge(tr_written, u + 1)
                    if u >= 2:
                        act.wait_ge(misc_written, misc_no[("pv", u - 2)] + 1)
                    copy(pT[:, u % 2, :, :], TR[u % 2][:, :].rearrange("p (j q) -> p j q", j=HP)).then_inc(tr_read, 1)

            def widen_k(s):
                widen(act, "scalar", s)

            def sum_magnitudes(s):
                if s in ABS_SLOTS:
                    w = ABS_SLOTS.index(s)
                    act.wait_ge(wf_in[w], 16)
                    nc.scalar.activation(tern[:, w, :], wf_sb[:, w, :], ACT.Abs,
                                         accum_out=asum[:, w:w + 1]).then_inc(asum_ready, 1)

            def ternary_signs(s):
                for i in range(3 * NPIECE):
                    if s == SIGN_SLOTS[i]:
                        act.wait_ge(w_int_ready, i + 1)
                        w, c = divmod(i, NPIECE)
                        cols = slice(PIECE * c, PIECE * c + PIECE)
                        nc.scalar.activation(tern[:, w, cols], wf_sb[:, w, cols], ACT.Sign,
                                             bias=minus_magic[:, :]).then_inc(tern_ready, 1)

            def silu_gate(s, c):
                t = s - GU0
                if 0 <= t < NT:
                    act.wait_ge(gu_scale_ready, t + 1)
                    j = 4 * t + 2 * c
                    act.wait_ge(gu_written, j + 1)
                    if t >= 2:
                        act.wait_ge(h_ready, NG * (t - 2) + c + 1)
                    nc.scalar.activation(g_sb[:, t % 2, GC * c:GC * c + GC], SC[j % 3][:, :], ACT.Silu,
                                         scale=s_out[:, 0, t:t + 1]).then_inc(silu_ready, 1)

            def read_gated(s, c):
                t = s - HT0
                if 0 <= t < NT:
                    n = NU + NG * t + c
                    act.wait_ge(tr_written, n + 1)
                    if t >= 2 and c == 0:
                        act.wait_ge(misc_written, misc_no[("dn", t - 2)] + 1)
                    copy(hT[:, t % 2, HC * c:HC * c + HC, :], TR[n % 2][:, :].rearrange("p (j q) -> p j q", j=HC),
                         bias=-MAGIC).then_inc(tr_read, 1)

            def scale_down_product(s):
                t = s - DN0
                if 0 <= t < NT and FINISHER[t] != "vector":
                    n = misc_no[("dn", t)]
                    act.wait_ge(misc_written, n + 1)
                    act.wait_ge(dn_scale_ready, t + 1)
                    nc.scalar.activation(o_sb[:, t, :], MI[n % 3][:, 0:C], ACT.Copy,
                                         scale=s_out[:, 2, t:t + 1]).then_inc(misc_read[n % 3], 1)

            for s in range(FFN_SLOT):
                exponentials(s)
                read_probabilities(s)
                read_misc_banks(s)
                ternary_signs(s)
                sum_magnitudes(s)
                widen_k(s)
            for s in range(FFN_SLOT, SLOTS):
                read_probabilities(s)
                exponentials(s)
                read_misc_banks(s)
                silu_gate(s, 0)
                silu_gate(s, 1)
                load_silu_tables(s)
                read_gated(s, 0)
                read_gated(s, 1)
                scale_down_product(s)

        @block.vector
        def _(dve):
            def copy(dst, src, scale=None, bias=None):
                if bias is not None:
                    return nc.vector.tensor_scalar(dst, src, 1.0, bias, ALU.mult, ALU.add)
                if scale is not None:
                    return nc.vector.tensor_scalar(dst, src, scale, 1.0, ALU.mult, ALU.mult)
                return nc.vector.tensor_copy(dst, src)

            nc.vector.memset(table_in[:, :], 0.0).then_inc(table_in_ready, 1)
            nc.vector.memset(warm[:, :], 0.0).then_inc(warm_ready, 1)
            nc.vector.memset(wkvT[L:, :], 0.0)
            for par in range(2):
                for half in range(2):
                    nc.vector.memset(parity_mask[Q * half:Q * half + Q, par:par + 1], float(par == half))
            nc.vector.memset(ctxT[L:, :], 0.0)
            nc.vector.memset(minus_magic[:, :], -MAGIC)
            nc.vector.memset(qT[:, :, :, S:], 0.0)
            nc.vector.memset(ctxT[0:L, T:], 0.0)
            nc.vector.memset(p_norm[:, :, :, S:], 0.0).then_inc(pads_ready, 1)

            def ln1_moments(first, last):
                for t in range(first, last):
                    dve.wait_ge(x_in[x_part(t)], 16)
                    nc.vector.bn_stats(stats[:, t, :], x_sb[:, t, :]).then_inc(stats_ready, 1)
                for t in range(first, last):
                    dve.wait_ge(stats_ready, t + 1)
                    nc.vector.bn_aggr(mv[:, t, :], stats[:, t, :]).then_inc(mv_ready, 1)

            def scores_of(u):
                return SC[u % 3][:, 0:HH * S].rearrange("p (h k) -> p h k", h=HH)

            ln1_moments(0, 2)
            ln1_moments(2, 4)
            nc.vector.memset(mean_w[:, :], 1.0 / WN).then_inc(pads_ready, 1)
            read_misc_jobs(dve, copy, "vector", -1)
            widen(dve, "vector", -1)

            def read_misc_banks(s):
                read_misc_jobs(dve, copy, "vector", s)

            def score_maxima(s):
                u = s
                if u < NU:
                    dve.wait_ge(scores_written, u + 1)
                    nc.vector.tensor_reduce(mx[:, u % R, :], scores_of(u), axis=AX_X, op=ALU.max).then_inc(max_ready, 1)

            def subtract_maxima(s):
                u = s
                if u < NU:
                    dve.wait_ge(max_ready, u + 1)
                    if u >= R:
                        dve.wait_ge(pn_ready, u - R + 1)
                    nc.vector.tensor_tensor(soft[:, u % R, :, :], scores_of(u),
                                            mx[:, u % R, :, None].to_broadcast([P, HH, S]),
                                            ALU.subtract).then_inc(sub_ready, 1)

            def sum_exponentials(s):
                u = s - 1
                if 0 <= u < NU:
                    dve.wait_ge(exp_ready, u + 1)
                    nc.vector.tensor_reduce(den[:, u % R, :], soft[:, u % R, :, :], axis=AX_X,
                                            op=ALU.add).then_inc(den_ready, 1)

            def invert_sums(s):
                u = s - 1
                if 0 <= u < NU:
                    dve.wait_ge(den_ready, u + 1)
                    nc.vector.reciprocal(rden[:, u % R, :], den[:, u % R, :]).then_inc(rden_ready, 1)

            def first_moments(s):
                for i, at in enumerate(LN1_SLOTS):
                    if s == at:
                        ln1_moments(4 + i, 5 + i)

            def widen_k(s):
                widen(dve, "vector", s)

            def add_attention(s):
                if s in OP_AT:
                    t = OP_AT[s]
                    n = misc_no[("op", t)]
                    dve.wait_ge(misc_written, n + 1)
                    nc.vector.tensor_tensor(x_sb[:, t, :], MI[n % 3][:, 0:C], x_sb[:, t, :],
                                            ALU.add).then_inc(misc_read[n % 3], 1)

            def second_stats(s):
                if s in OP_AT:
                    t = OP_AT[s]
                    wait_read(dve, ("op", t))
                    nc.vector.bn_stats(stats[:, NT + t, :], x_sb[:, t, :]).then_inc(stats_ready, 1)

            def second_moments(s):
                if s in OP_AT:
                    t = OP_AT[s]
                    dve.wait_ge(stats_ready, NT + t + 1)
                    nc.vector.bn_aggr(mv[:, NT + t, :], stats[:, NT + t, :]).then_inc(mv_ready, 1)

            def token_maxima(s):
                if s in Y_AT:
                    t = Y_AT[s]
                    dve.wait_ge(yn_ready, t + 1)
                    nc.vector.tensor_reduce(amax[:, 0, t:t + 1], y_sb[:, t % 2, :], axis=AX_X, op=ALU.max,
                                            apply_absolute_value=True).then_inc(y_amax_ready, 1)

            def token_scales(s):
                if s in Y_AT:
                    t = Y_AT[s]
                    dve.wait_ge(y_amax_ready, t + 1)
                    nc.vector.tensor_scalar(s_tok[:, 0, t:t + 1], amax[:, 0, t:t + 1], 1.0 / 127.0, EPS,
                                            ALU.mult, ALU.add).then_inc(y_scale_ready, 1)

            def invert_token_scales(s):
                if s in Y_AT:
                    t = Y_AT[s]
                    dve.wait_ge(y_scale_ready, t + 1)
                    nc.vector.reciprocal(r_tok[:, 0, t:t + 1], s_tok[:, 0, t:t + 1]).then_inc(y_ready, 1)

            def gate_up_scales(s):
                if s in Y_AT:
                    t = Y_AT[s]
                    dve.wait_ge(y_scale_ready, t + 1)
                    wait_read(dve, ("mean", 0), ("mean", 1))
                    nc.vector.tensor_scalar(s_out[:, 0:2, t], w_scale[:, 0:2], s_tok[:, 0, t:t + 1], None,
                                            ALU.mult).then_inc(gu_scale_ready, 1)

            def invert_weight_scale(s):
                for w in range(3):
                    if s == INVERSE_SLOTS[w]:
                        wait_read(dve, ("mean", w))
                        nc.vector.reciprocal(w_inv[:, w:w + 1], w_scale[:, w:w + 1]).then_inc(w_inv_ready, 1)

            def gate_times_up(s, c):
                t = s - GU0
                if 0 <= t < NT:
                    j = 4 * t + 2 * c + 1
                    cols = slice(GC * c, GC * c + GC)
                    dve.wait_ge(gu_written, j + 1)
                    dve.wait_ge(silu_ready, NG * t + c + 1)
                    if t >= 3:
                        dve.wait_ge(*rounded(t - 3, c))
                    nc.vector.scalar_tensor_tensor(h_sb[:, t % 3, cols], SC[j % 3][:, :], s_out[:, 1, t:t + 1],
                                                   g_sb[:, t % 2, cols], ALU.mult, ALU.mult).then_inc(h_ready, 1)

            def gated_maxima(s):
                t = s - GU0
                if 0 <= t < NT:
                    dve.wait_ge(h_ready, NG * (t + 1))
                    nc.vector.tensor_reduce(amax[:, 1, t:t + 1], h_sb[:, t % 3, :], axis=AX_X, op=ALU.max,
                                            apply_absolute_value=True).then_inc(h_amax_ready, 1)

            def gated_scales(s):
                t = s - GU0
                if 0 <= t < NT:
                    dve.wait_ge(h_amax_ready, t + 1)
                    nc.vector.tensor_scalar(s_tok[:, 1, t:t + 1], amax[:, 1, t:t + 1], 1.0 / 127.0, EPS,
                                            ALU.mult, ALU.add).then_inc(h_scale_ready, 1)

            def invert_gated_scales(s):
                t = s - GU0
                if 0 <= t < NT:
                    dve.wait_ge(h_scale_ready, t + 1)
                    nc.vector.reciprocal(r_tok[:, 1, t:t + 1], s_tok[:, 1, t:t + 1]).then_inc(r_ready, 1)
                    nc.vector.tensor_tensor(s_out[:, 2, t:t + 1], s_tok[:, 1, t:t + 1], w_scale[:, 2:3],
                                            ALU.mult).then_inc(dn_scale_ready, 1)

            def round_gated(s, c):
                t = s - GU0
                if 0 <= t < NT:
                    round_h(dve, nc.vector, "vector", t, c)

            def add_down_product(s):
                t = s - DN0
                if 0 <= t < NT:
                    if FINISHER[t] != "vector":
                        return
                    n = misc_no[("dn", t)]
                    dve.wait_ge(misc_written, n + 1)
                    dve.wait_ge(dn_scale_ready, t + 1)
                    nc.vector.scalar_tensor_tensor(o_sb[:, t, :], MI[n % 3][:, 0:C], s_out[:, 2, t:t + 1],
                                                   x_sb[:, t, :], ALU.mult, ALU.add).then_inc(misc_read[n % 3], 1)

            for s in range(FFN_SLOT):
                read_misc_banks(s)
                first_moments(s)
                score_maxima(s)
                sum_exponentials(s)
                subtract_maxima(s)
                token_maxima(s)
                invert_sums(s)
                invert_weight_scale(s)
                widen_k(s)
                add_attention(s)
                second_stats(s)
                second_moments(s)
                token_scales(s)
                gate_up_scales(s)
                invert_token_scales(s)
            for s in range(FFN_SLOT, SLOTS):
                read_misc_banks(s)
                sum_exponentials(s)
                invert_sums(s)
                add_attention(s)
                gate_times_up(s, 0)
                gate_times_up(s, 1)
                second_stats(s)
                gated_maxima(s)
                second_moments(s)
                gated_scales(s)
                token_maxima(s)
                invert_gated_scales(s)
                round_gated(s, 0)
                round_gated(s, 1)
                add_down_product(s)
                token_scales(s)
                gate_up_scales(s)
                invert_token_scales(s)

        @block.tensor
        def _(pe):
            def mm(*a, **k):
                return nc.tensor.matmul(*a, **k)

            def write_misc(job):
                n = misc_no[job]
                kind, i = job[0], job[1]
                bank = MI[n % 3]
                if n >= 3:
                    pe.wait_ge(misc_read[n % 3], n // 3)
                if kind == "wkvT":
                    const(pe, "ident")
                    pe.wait_ge(wkv_in, 16)
                    for o in range(4):
                        last = nc.tensor.transpose(bank[0:L, P * o:P * o + P], wkv_sb[:, o, :], ident[:, :])
                elif kind == "ctxT":
                    pe.wait_ge(ctx_in[i], 32)
                    for j in range(4):
                        last = nc.tensor.transpose(bank[0:L, 2 * S * j:2 * S * j + 2 * S], ctx_sb[:, 4 * i + j, :],
                                                   ident[0:2 * S, 0:2 * S])
                elif kind == "k":
                    hf = job[2]
                    wait_read(pe, ("wkvT", 0), ("ctxT", i))
                    pe.wait_ge(pads_ready, 1)
                    last = mm(bank[:, 0:KT], wkvT[:, P * hf:P * hf + P], ctxT[:, KT * i:KT * i + KT],
                              start=True, stop=True)
                elif kind in ("wqT", "woT"):
                    pe.wait_ge(wq_in if kind == "wqT" else wo_in, 16)
                    w = wq_sb if kind == "wqT" else wo_sb
                    for a in range(HALVES):
                        for o in range(HALVES):
                            last = nc.tensor.transpose(bank[:, C * a + P * o:C * a + P * o + P],
                                                       w[:, o, P * a:P * a + P], ident[:, :])
                elif kind == "xT":
                    pe.wait_ge(xn_ready, i + 1)
                    for a in range(HALVES):
                        last = nc.tensor.transpose(bank[:, P * a:P * a + P], xn_sb[:, i % 4, P * a:P * a + P],
                                                   ident[:, :])
                elif kind == "q":
                    t = (CT * (i + 1) - 1) // P
                    wait_read(pe, ("wqT", 0), *[("xT", n) for n in range(t + 1)])
                    for o in range(HALVES):
                        for a in range(HALVES):
                            last = mm(bank[:, CT * o:CT * o + CT], wqT[:, a, P * o:P * o + P],
                                      xnT[:, a, CT * i:CT * i + CT], start=(a == 0), stop=(a == HALVES - 1))
                elif kind == "v":
                    wait_read(pe, ("wkvT", 0), *[("ctxT", c) for c in range(NKC)])
                    wv = wkvT[:, C:2 * C].rearrange("l (h e d) -> l e h d", e=2, d=HD)
                    for b in range(VB):
                        c0 = S * (VB * i + b)
                        for par in range(2):
                            last = mm(bank[Q * par:Q * par + Q, P * b:P * b + P], ctxT[:, c0:c0 + Q], wv[:, par, :, :],
                                      start=True, stop=True)
                elif kind == "mean":
                    pe.wait_ge(pads_ready, 2)
                    pe.wait_ge(asum_ready, i + 1)
                    last = mm(bank[:, 0:1], mean_w[:, :], asum[:, i:i + 1], start=True, stop=True)
                elif kind == "pv":
                    p, hf = divmod(i, HALVES)
                    pe.wait_ge(tr_read, i + 1)
                    wait_read(pe, ("v", 2 * p // VB))
                    for par in range(2):
                        for j in range(HP):
                            last = mm(bank[32 * j:32 * j + 32, S * par:S * par + S],
                                      v_wide[:, 2 * p + par, HP * hf + j, :], pT[:, i % 2, j, Q * par:Q * par + S],
                                      start=True, stop=True)
                elif kind == "wT":
                    k = job[2]
                    pe.wait_ge(tern_ready, NPIECE * (i + 1))
                    const(pe, "ident_b")
                    b16 = bank[:, :].bitcast(BF16)
                    for c in range(NC8):
                        c0 = C * c + P * k if i < 2 else I * k + P * c
                        last = nc.tensor.transpose(b16[:, P * c:P * c + P], tern[:, i, c0:c0 + P], ident_b[:, :])
                elif kind == "xqT":
                    pe.wait_ge(yint_ready, i + 1)
                    for a in range(HALVES):
                        last = nc.tensor.transpose(bank[:, P * a:P * a + P], y_int[:, i % 2, P * a:P * a + P],
                                                   ident[:, :])
                last.then_inc(misc_written, 1)

            def scores(u):
                p, hf = divmod(u, HALVES)
                bank = SC[u % 3]
                if u >= 3:
                    pe.wait_ge(sub_ready, u - 2)
                if u == 0:
                    const(pe, "causal")
                    pe.wait_ge(pads_ready, 1)
                if p % 2 == 0 and hf == 0:
                    wait_read(pe, ("q", p // 2))
                if p % 4 == 0:
                    pe.wait_ge(kw_ready[p // 4][hf], HH)
                out_ = bank[:, 0:HH * S].rearrange("p (h k) -> p h k", h=HH)
                mm(out_, sel2[:, :], causal[:, None, :].to_broadcast([P, HH, S]), start=True, stop=False)
                for par in range(2):
                    c0 = S * (2 * p + par)
                    last = mm(out_[Q * par:Q * par + Q, :, :], qT[:, hf, 2 * p + par, :], k_wide[:, hf, :, c0:c0 + S],
                              start=False, stop=True)
                last.then_inc(scores_written, 1)

            def gate_up(s, c):
                t = s - GU0
                if 0 <= t < NT:
                    for w in range(2):
                        j = 4 * t + 2 * c + w
                        if j == 0:
                            pe.wait_ge(sub_ready, NU)
                            wait_read(pe, *[("wT", w, k) for w in range(2) for k in range(2)])
                        if j >= 3:
                            pe.wait_ge((silu_ready, h_ready)[(j - 3) % 2], (j - 3) // 2 + 1)
                        if c == 0 and w == 0:
                            wait_read(pe, ("xqT", t))
                        for a in range(HALVES):
                            last = mm(SC[j % 3][:, :], xqT[:, t, a, :], wT[:, w, a, GC * c:GC * c + GC],
                                      start=(a == 0), stop=(a == HALVES - 1))
                        last.then_inc(gu_written, 1)

            pe.wait_ge(warm_ready, 1)
            for _ in range(WARM_PRODUCTS):
                mm(MI[2][:, :], warm[:, 0:P], warm[:, :], start=True, stop=True)
            for job in misc[-1]:
                write_misc(job)

            def score_unit(s):
                if s < NU:
                    scores(s)

            def transpose_probabilities(s):
                u = s - LAG_T
                if 0 <= u < NU:
                    pe.wait_ge(pn_ready, u + 1)
                    if u >= 2:
                        pe.wait_ge(tr_read, u - 1)
                    for j in range(HP):
                        last = nc.tensor.transpose(TR[u % 2][:, P * j:P * j + P],
                                                   p_norm[:, u % R, 2 * j:2 * j + 2, :].rearrange("p h k -> p (h k)"),
                                                   ident[:, :])
                    last.then_inc(tr_written, 1)

            def misc_products(s):
                for job in misc[s]:
                    write_misc(job)

            def output_projection(s):
                if s in OP_AT:
                    t = OP_AT[s]
                    need = (P * (t + 1) - 1) // (2 * S)
                    wait_read(pe, ("woT", 0), *[("pv", u) for u in range(HALVES * (need + 1))])
                    n = misc_no[("op", t)]
                    pe.wait_ge(misc_read[n % 3], n // 3)
                    for a in range(HALVES):
                        last = mm(MI[n % 3][:, 0:C], attnT[:, a, P * t:P * t + P], woT[:, a, :],
                                  start=(a == 0), stop=(a == HALVES - 1))
                    last.then_inc(misc_written, 1)

            def transpose_gated(s, h):
                t = s - HT0
                if 0 <= t < NT:
                    n = NU + NG * t + h
                    pe.wait_ge(*rounded(t, h))
                    pe.wait_ge(tr_read, n - 1)
                    for c in range(HC):
                        last = nc.tensor.transpose(TR[n % 2][:, P * c:P * c + P],
                                                   h_int[:, t % 2, h, P * c:P * c + P], ident[:, :])
                    last.then_inc(tr_written, 1)

            def down_projection(s):
                t = s - DN0
                if 0 <= t < NT:
                    n = misc_no[("dn", t)]
                    pe.wait_ge(misc_read[n % 3], n // 3)
                    if t == 0:
                        wait_read(pe, ("wT", 2, 0), ("wT", 2, 1))
                    for c in range(NC8):
                        if c % HC == 0:
                            pe.wait_ge(tr_read, NU + NG * t + c // HC + 1)
                        last = mm(MI[n % 3][:, 0:C], hT[:, t % 2, c, :], wdT[:, c, :],
                                  start=(c == 0), stop=(c == NC8 - 1))
                    last.then_inc(misc_written, 1)

            for s in range(FFN_SLOT):
                score_unit(s)
                transpose_probabilities(s)
                output_projection(s)
                misc_products(s)
            for s in range(FFN_SLOT, SLOTS):
                output_projection(s)
                transpose_probabilities(s)
                misc_products(s)
                gate_up(s, 0)
                gate_up(s, 1)
                transpose_gated(s, 0)
                transpose_gated(s, 1)
                down_projection(s)

_INS = ["x", "ctx_512", "L0_xattn_Wq", "L0_xattn_Wkv_expand", "L0_xattn_Wout",
        "L0_ffn_w_gate", "L0_ffn_w_up", "L0_ffn_w_down"]
_OUTS = [((16, 56, 256), "float32")]


def kernel(**inputs):
    import numpy as _np
    import concourse.bacc as _bacc
    from concourse import mybir as _mybir
    from concourse.bass_utils import run_bass_kernel_spmd as _run

    nc = _bacc.Bacc("TRN2", target_bir_lowering=False, num_devices=1)
    arrays, args = {}, []
    for name in _INS:
        a = _np.ascontiguousarray(inputs[name])
        arrays[f"in_{name}_dram"] = a
        args.append(nc.dram_tensor(f"in_{name}_dram", a.shape, _mybir.dt.from_np(a.dtype), kind="ExternalInput").ap())
    for i, (shape, dtype) in enumerate(_OUTS):
        dt = _mybir.dt.from_np(_np.dtype(dtype))
        args.append(nc.dram_tensor(f"out_{i}_dram", shape, dt, kind="ExternalOutput").ap())
    xattn_ffn(nc, *args)
    r = _run(nc, [arrays], core_ids=[0])
    return r.results[0]["out_0_dram"]
```
